# Optimizing a Trainium2 kernel written in Bass

```python
import numpy as np
import jax
import jax.numpy as jnp

def _softmax(x, axis=-1):
    return jax.nn.softmax(x, axis=axis)

def _gelu(x):
    return jax.nn.gelu(x, approximate=True)

def _silu(x):
    return jax.nn.silu(x)

def _sigmoid(x):
    return jax.nn.sigmoid(x)

def _layernorm(x, axis=-1, eps=1e-05):
    m = jnp.mean(x, axis=axis, keepdims=True)
    v = jnp.var(x, axis=axis, keepdims=True)
    return (x - m) / jnp.sqrt(v + eps)

def _scatter_add(tgt, idx, src, axis=0):
    return tgt.at[idx].add(src)

def _segment_sum(src, seg, n):
    return jax.ops.segment_sum(src, seg, n)
kernel_name = 'mk_seq_postln_d1_jaxref_r2_b70940'

def setup_inputs(seed: int=0):
    np.random.seed(seed)
    _w = jnp.asarray

    def _L0_attn_setup():
        import jax, jax.numpy as jnp
        import numpy as np
        D_STATE = 16
        DT_RANK = 32
        D_CONV = 4

        def _mamba(x, in_w, conv_w, conv_b, xproj_w, dt_w, dt_b, A_log, Dp, out_w):
            Bn, L, _ = x.shape
            di = in_w.shape[0] // 2
            xz = jnp.einsum('bld,ed->ble', x, in_w)
            xh, z = jnp.split(xz, 2, axis=-1)
            xp = jnp.pad(xh, ((0, 0), (D_CONV - 1, 0), (0, 0)))
            k = conv_w.T[:, None, :]
            xc = jax.lax.conv_general_dilated(xp, k, (1,), 'VALID', dimension_numbers=('NWC', 'WIO', 'NWC'), feature_group_count=di) + conv_b
            xc = jax.nn.silu(xc)
            dbc = jnp.einsum('bld,ed->ble', xc, xproj_w)
            dt, Bm, Cm = jnp.split(dbc, [DT_RANK, DT_RANK + D_STATE], axis=-1)
            delta = jax.nn.softplus(jnp.einsum('blr,dr->bld', dt, dt_w) + dt_b)
            A = -jnp.exp(A_log)
            dA = jnp.exp(delta[..., None] * A)
            dBu = delta[..., None] * Bm[:, :, None, :] * xc[..., None]

            def step(h, inp):
                dA_t, dBu_t, C_t = inp
                h = h * dA_t + dBu_t
                return (h, jnp.einsum('bds,bs->bd', h, C_t))
            h0 = jnp.zeros((Bn, di, D_STATE), x.dtype)
            _, ys = jax.lax.scan(step, h0, (jnp.swapaxes(dA, 0, 1), jnp.swapaxes(dBu, 0, 1), jnp.swapaxes(Cm, 0, 1)))
            y = jnp.swapaxes(ys, 0, 1) + xc * Dp
            y = y * jax.nn.silu(z)
            return jnp.einsum('bld,od->blo', y, out_w)

        def _reference_tuple_inner(x, in_w1, conv_w1, conv_b1, xproj_w1, dt_w1, dt_b1, A_log1, D1, out_w1, in_w2, conv_w2, conv_b2, xproj_w2, dt_w2, dt_b2, A_log2, D2, out_w2):
            dm = x.shape[-1] // 2
            residual = x
            fwd = x[..., :dm]
            bwd = jnp.flip(x[..., dm:], axis=1)
            h1 = _mamba(fwd, in_w1, conv_w1, conv_b1, xproj_w1, dt_w1, dt_b1, A_log1, D1, out_w1)
            h2 = _mamba(bwd, in_w2, conv_w2, conv_b2, xproj_w2, dt_w2, dt_b2, A_log2, D2, out_w2)
            hidden = jnp.concatenate([h1, h2], axis=-1)
            return (hidden, residual)
        key = jax.random.key(seed)
        B, L, dim = (2, 1024, 512)
        dm = dim // 2
        di = 2 * dm
        kx, k1, k2 = jax.random.split(key, 3)

        def w(k, shape, s=0.02):
            return jax.random.normal(k, shape, jnp.float32) * s

        def params(kk, tag):
            k = jax.random.split(kk, 5)
            dt_init = float(np.log(np.expm1(0.01)))
            return {f'in_w{tag}': w(k[0], (2 * di, dm)), f'conv_w{tag}': w(k[1], (di, D_CONV), 0.2), f'conv_b{tag}': jnp.zeros((di,), jnp.float32), f'xproj_w{tag}': w(k[2], (DT_RANK + 2 * D_STATE, di)), f'dt_w{tag}': w(k[3], (di, DT_RANK), 0.1), f'dt_b{tag}': jnp.full((di,), dt_init, jnp.float32), f'A_log{tag}': jnp.log(jnp.broadcast_to(jnp.arange(1, D_STATE + 1, dtype=jnp.float32), (di, D_STATE))), f'D{tag}': jnp.ones((di,), jnp.float32), f'out_w{tag}': w(k[4], (dm, di))}
        inp = {'x': jax.random.normal(kx, (B, L, dim), jnp.float32)}
        inp.update(params(k1, '1'))
        inp.update(params(k2, '2'))
        return inp
    _L0_attn_in = _L0_attn_setup()

    def _L0_ffn_setup():
        import jax, jax.numpy as jnp
        import numpy as np
        DIM = 512
        HIDDEN = 1536
        SCALE = 1.0 / 127.0

        def _dequant(w_int, dtype):
            return w_int.astype(dtype) * jnp.asarray(SCALE, dtype)
        key = jax.random.key(seed)
        k_x, k_g, k_u, k_d = jax.random.split(key, 4)
        x = jax.random.normal(k_x, (4, 1024, DIM), dtype=jnp.float32)
        w_gate = jax.random.randint(k_g, (HIDDEN, DIM), -127, 128, dtype=jnp.int32)
        w_up = jax.random.randint(k_u, (HIDDEN, DIM), -127, 128, dtype=jnp.int32)
        w_down = jax.random.randint(k_d, (DIM, HIDDEN), -127, 128, dtype=jnp.int32)
        return {'x': x, 'w_gate': w_gate, 'w_up': w_up, 'w_down': w_down}
    _L0_ffn_in = _L0_ffn_setup()
    _d = {'L0_attn_x': _L0_attn_in['x'], 'L0_attn_in_w1': _L0_attn_in['in_w1'], 'L0_attn_conv_w1': _L0_attn_in['conv_w1'], 'L0_attn_conv_b1': _L0_attn_in['conv_b1'], 'L0_attn_xproj_w1': _L0_attn_in['xproj_w1'], 'L0_attn_dt_w1': _L0_attn_in['dt_w1'], 'L0_attn_dt_b1': _L0_attn_in['dt_b1'], 'L0_attn_A_log1': _L0_attn_in['A_log1'], 'L0_attn_D1': _L0_attn_in['D1'], 'L0_attn_out_w1': _L0_attn_in['out_w1'], 'L0_attn_in_w2': _L0_attn_in['in_w2'], 'L0_attn_conv_w2': _L0_attn_in['conv_w2'], 'L0_attn_conv_b2': _L0_attn_in['conv_b2'], 'L0_attn_xproj_w2': _L0_attn_in['xproj_w2'], 'L0_attn_dt_w2': _L0_attn_in['dt_w2'], 'L0_attn_dt_b2': _L0_attn_in['dt_b2'], 'L0_attn_A_log2': _L0_attn_in['A_log2'], 'L0_attn_D2': _L0_attn_in['D2'], 'L0_attn_out_w2': _L0_attn_in['out_w2'], 'L0_ffn_w_gate': _L0_ffn_in['w_gate'], 'L0_ffn_w_up': _L0_ffn_in['w_up'], 'L0_ffn_w_down': _L0_ffn_in['w_down']}
    _x0 = _d['L0_attn_x']
    _d['L0_attn_x'] = jax.random.normal(jax.random.fold_in(jax.random.key(seed), 1), (1, 8192, 512), dtype=_x0.dtype)
    del _x0
    return _d

def reference(L0_attn_x, L0_attn_in_w1, L0_attn_conv_w1, L0_attn_conv_b1, L0_attn_xproj_w1, L0_attn_dt_w1, L0_attn_dt_b1, L0_attn_A_log1, L0_attn_D1, L0_attn_out_w1, L0_attn_in_w2, L0_attn_conv_w2, L0_attn_conv_b2, L0_attn_xproj_w2, L0_attn_dt_w2, L0_attn_dt_b2, L0_attn_A_log2, L0_attn_D2, L0_attn_out_w2, L0_ffn_w_gate, L0_ffn_w_up, L0_ffn_w_down):

    def _L0_attn_ref(x, in_w1, conv_w1, conv_b1, xproj_w1, dt_w1, dt_b1, A_log1, D1, out_w1, in_w2, conv_w2, conv_b2, xproj_w2, dt_w2, dt_b2, A_log2, D2, out_w2):
        import jax, jax.numpy as jnp
        import numpy as np
        D_STATE = 16
        DT_RANK = 32
        D_CONV = 4

        def _mamba(x, in_w, conv_w, conv_b, xproj_w, dt_w, dt_b, A_log, Dp, out_w):
            Bn, L, _ = x.shape
            di = in_w.shape[0] // 2
            xz = jnp.einsum('bld,ed->ble', x, in_w)
            xh, z = jnp.split(xz, 2, axis=-1)
            xp = jnp.pad(xh, ((0, 0), (D_CONV - 1, 0), (0, 0)))
            k = conv_w.T[:, None, :]
            xc = jax.lax.conv_general_dilated(xp, k, (1,), 'VALID', dimension_numbers=('NWC', 'WIO', 'NWC'), feature_group_count=di) + conv_b
            xc = jax.nn.silu(xc)
            dbc = jnp.einsum('bld,ed->ble', xc, xproj_w)
            dt, Bm, Cm = jnp.split(dbc, [DT_RANK, DT_RANK + D_STATE], axis=-1)
            delta = jax.nn.softplus(jnp.einsum('blr,dr->bld', dt, dt_w) + dt_b)
            A = -jnp.exp(A_log)
            dA = jnp.exp(delta[..., None] * A)
            dBu = delta[..., None] * Bm[:, :, None, :] * xc[..., None]

            def step(h, inp):
                dA_t, dBu_t, C_t = inp
                h = h * dA_t + dBu_t
                return (h, jnp.einsum('bds,bs->bd', h, C_t))
            h0 = jnp.zeros((Bn, di, D_STATE), x.dtype)
            _, ys = jax.lax.scan(step, h0, (jnp.swapaxes(dA, 0, 1), jnp.swapaxes(dBu, 0, 1), jnp.swapaxes(Cm, 0, 1)))
            y = jnp.swapaxes(ys, 0, 1) + xc * Dp
            y = y * jax.nn.silu(z)
            return jnp.einsum('bld,od->blo', y, out_w)

        def _reference_tuple_inner(x, in_w1, conv_w1, conv_b1, xproj_w1, dt_w1, dt_b1, A_log1, D1, out_w1, in_w2, conv_w2, conv_b2, xproj_w2, dt_w2, dt_b2, A_log2, D2, out_w2):
            dm = x.shape[-1] // 2
            residual = x
            fwd = x[..., :dm]
            bwd = jnp.flip(x[..., dm:], axis=1)
            h1 = _mamba(fwd, in_w1, conv_w1, conv_b1, xproj_w1, dt_w1, dt_b1, A_log1, D1, out_w1)
            h2 = _mamba(bwd, in_w2, conv_w2, conv_b2, xproj_w2, dt_w2, dt_b2, A_log2, D2, out_w2)
            hidden = jnp.concatenate([h1, h2], axis=-1)
            return (hidden, residual)
        return _reference_tuple_inner(x, in_w1, conv_w1, conv_b1, xproj_w1, dt_w1, dt_b1, A_log1, D1, out_w1, in_w2, conv_w2, conv_b2, xproj_w2, dt_w2, dt_b2, A_log2, D2, out_w2)[0]

    def _L0_ffn_ref(x, w_gate, w_up, w_down):
        import jax, jax.numpy as jnp
        import numpy as np
        DIM = 512
        HIDDEN = 1536
        SCALE = 1.0 / 127.0

        def _dequant(w_int, dtype):
            return w_int.astype(dtype) * jnp.asarray(SCALE, dtype)
        wg = _dequant(w_gate, x.dtype)
        wu = _dequant(w_up, x.dtype)
        wd = _dequant(w_down, x.dtype)
        gate = jnp.einsum('bsd,hd->bsh', x, wg)
        up = jnp.einsum('bsd,hd->bsh', x, wu)
        h = jax.nn.silu(gate) * up
        return jnp.einsum('bsh,dh->bsd', h, wd)
    x = L0_attn_x
    x = _layernorm(x + _L0_attn_ref(x, L0_attn_in_w1, L0_attn_conv_w1, L0_attn_conv_b1, L0_attn_xproj_w1, L0_attn_dt_w1, L0_attn_dt_b1, L0_attn_A_log1, L0_attn_D1, L0_attn_out_w1, L0_attn_in_w2, L0_attn_conv_w2, L0_attn_conv_b2, L0_attn_xproj_w2, L0_attn_dt_w2, L0_attn_dt_b2, L0_attn_A_log2, L0_attn_D2, L0_attn_out_w2), axis=-1)
    x = _layernorm(x + _L0_ffn_ref(x, L0_ffn_w_gate, L0_ffn_w_up, L0_ffn_w_down), axis=-1)
    return x

_drawn_inputs = setup_inputs


def setup_inputs(seed=0):
    import zlib

    import numpy as np

    out = dict(_drawn_inputs(seed))
    spreads = {'L0_attn_conv_b1': (0.0, 0.8),
     'L0_attn_dt_b1': (-4.600165843963623, 0.6),
     'L0_attn_D1': (1.0, 0.6),
     'L0_attn_conv_b2': (0.0, 0.8),
     'L0_attn_dt_b2': (-4.600165843963623, 0.6),
     'L0_attn_D2': (1.0, 0.6)}
    factors = {'L0_attn_in_w1': 8.0,
     'L0_attn_conv_w1': 8.0,
     'L0_attn_xproj_w1': 8.0,
     'L0_attn_dt_w1': 8.0,
     'L0_attn_A_log1': 8.0,
     'L0_attn_out_w1': 8.0,
     'L0_attn_in_w2': 8.0,
     'L0_attn_conv_w2': 8.0,
     'L0_attn_xproj_w2': 8.0,
     'L0_attn_dt_w2': 8.0,
     'L0_attn_A_log2': 8.0,
     'L0_attn_out_w2': 8.0}
    for name, (base, spread) in spreads.items():
        noise = np.random.default_rng([zlib.crc32(name.encode()), seed]).standard_normal(out[name].shape)
        drawn = base * np.exp(spread * noise) if base else spread * noise
        out[name] = jnp.asarray(drawn.astype(out[name].dtype))
    for name, factor in factors.items():
        out[name] = (out[name] * factor).astype(out[name].dtype)
    return out
```

```python
from contextlib import ExitStack

import concourse.bass as bass
from concourse import mybir

ALU = mybir.AluOpType
ACT = mybir.ActivationFunctionType
F32 = mybir.dt.float32
I32 = mybir.dt.int32

P = 128
T = 256
TB = T // P
NS = 16
NQ = 2
TAPS = 4
EPS = 1e-5
WEIGHT_SCALE = 1.0 / 127.0

LOG1P_LEAD = 0.005232691452828611
LOG1P_FACTORS = [(-2.3216866366639644, 0.43240686292846314), (-1.4247358216099517, 2.702103630824708),
                 (1.009357722539173, 1.1060623827831724), (-0.08225184120489804, 3.257468775834742)]
NF = len(LOG1P_FACTORS)

JOBS = {
    0: [("Y0", 1, "fin"), ("Y1", 0, "fin"), ("X0", 1, "front"), ("X1", 0, "front"), ("O", 1, "fin"),
        ("Z0", 0, "scan"), ("Z1", 1, "scan"), ("T0", 0, "ffn"), ("T1", 1, "ffn"), ("P", 0, "front"),
        ("G0", 1, "ffn"), ("D0", 0, "front"), ("G1", 0, "ffn"), ("D1", 1, "front"), ("G2", 0, "ffn"),
        ("G3", 1, "ffn"), ("G4", 0, "ffn"), ("G5", 1, "ffn"), ("G6", 0, "ffn")],
    1: [("Y0", 0, "fin"), ("Y1", 1, "fin"), ("X0", 0, "front"), ("X1", 1, "front"), ("G7", 0, "ffn"),
        ("O", 1, "fin"), ("Z0", 0, "scan"), ("Z1", 1, "scan"), ("G8", 0, "ffn"), ("G9", 1, "ffn"),
        ("G10", 0, "ffn"), ("G11", 1, "ffn"), ("P", 0, "front"), ("W0", 1, "ffn"), ("D0", 0, "front"),
        ("D1", 0, "front"), ("W1", 0, "ffn")],
}


def parts_of(c, h, chunks):
    if c < 0:
        return {"front"} if h == 1 else set()
    if c >= chunks:
        return {0: {"fin", "ffn"}, 1: {"ffn"}}[h]
    parts = {"scan"}
    if c > 0 or h == 1:
        parts.add("fin")
    if c > 0:
        parts.add("ffn")
    if c < chunks - 1 or h == 0:
        parts.add("front")
    return parts


def jobs_of(c, h, chunks):
    return [(name, bank) for name, bank, part in JOBS[h] if part in parts_of(c, h, chunks)]


def used_before(c, bank, chunks):
    known = c if isinstance(c, int) else 2
    n = sum(b == bank for k in range(-1, known) for h in (0, 1) for _, b in jobs_of(k, h, chunks))
    if isinstance(c, int):
        return n
    per_step = sum(b == bank for h in (0, 1) for _, b in jobs_of(2, h, chunks))
    return (c - 2) * per_step + n


class MiscJob:

    def __init__(self, c, h, name, chunks):
        sort_c = c if isinstance(c, int) else 2
        listed = [(k, n, b) for k in (0, 1) for n, b in jobs_of(sort_c, k, chunks)]
        at = [(k, n) for k, n, _ in listed].index((h, name))
        self.bank = listed[at][2]
        self.before = used_before(c, self.bank, chunks) + sum(b == self.bank for _, _, b in listed[:at])


def mamba_pair_ffn_kernel(nc, xT, x, in_wT, conv_w, conv_b, xproj_wT, dt_wT, dt_b, A_log, Dp, out_wT,
                          w_gateT, w_upT, w_downT, ident_in, out):
    L, DIM = x.shape
    DM = DIM // NQ
    KM = DM // P
    DI = in_wT[0].shape[1] // 2
    DT = DI // P
    R = dt_wT[0].shape[0]
    KD = DIM // P
    HID = w_gateT.shape[1]
    FT = HID // P
    CH = L // T
    NG = 4
    SG = 2
    GROUPS = NS // SG
    assert L % T == 0 and CH >= 4 and DT == 4 and KM == 2 and TB == 2 and FT == 12 and KD == 4

    b_scratch = nc.dram_tensor("b_scratch", [NQ, NS, T], F32).ap()

    with ExitStack() as ctx:
        def sb(name, shape, dt=F32):
            return ctx.enter_context(nc.sbuf_tensor(name, shape, dt))

        def sem(name):
            return ctx.enter_context(nc.semaphore(name))

        in_w = sb("in_w", [P, NQ, KM, 2 * DI])
        xproj_w = sb("xproj_w", [P, NQ, DT, R + 2 * NS])
        dt_w = sb("dt_w", [R, NQ, DI])
        out_w = sb("out_w", [P, NQ, DT, DM])
        gate_w = sb("gate_w", [P, KD, HID])
        up_w = sb("up_w", [P, KD, HID])
        down_w = sb("down_w", [P, FT, DIM])
        ident = sb("ident", [P, P])
        conv_ws = sb("conv_ws", [P, NQ, DT, TAPS])
        conv_bs = sb("conv_bs", [P, NQ, DT])
        dt_bs = sb("dt_bs", [P, NQ, DT])
        a_neg = sb("a_neg", [P, NQ, DT, NS])
        d_skip = sb("d_skip", [P, NQ, DT])
        b_rows = sb("b_rows", [P, NG, SG, T])
        dbu = sb("dbu", [P, 2, DT, T])
        h = sb("h", [P, 2, DT, T])
        carry = sb("carry", [P, NQ, NS, DT])
        y_t = sb("y_t", [P, NQ, TB, DI])
        delta = sb("delta", [P, NQ, DT, T])
        du = sb("du", [P, NQ, DT, T])
        xc = sb("xc", [P, NQ, DT, T])
        c_t = sb("c_t", [P, NQ, TB, NS])
        x_in = sb("x_in", [P, NQ, KM, T])
        xh = sb("xh", [P, DT, TAPS - 1 + T])
        halo = sb("halo", [P, NQ, DT, TAPS - 1])
        tmp4 = sb("tmp4", [P, 4, T])
        th_x = sb("th_x", [P, 2, T])
        dt_sb = sb("dt_sb", [R + NS, T])
        zs = sb("zs", [P, DT, T])
        res = sb("res", [P, TB, DIM])
        xn = sb("xn", [P, TB, DIM])
        xnT = sb("xnT", [P, KD, T])
        th_g = sb("th_g", [P, 2, T])
        up_f = sb("up_f", [P, 2, T])
        hid = sb("hid", [P, FT, T])
        stats = sb("stats", [P, 2, TB, 6])
        mv = sb("mv", [P, 2, TB, 2])
        rstd = sb("rstd", [P, 2, TB])
        negm = sb("negm", [P, 2, TB])
        shift = sb("shift", [P, 2, TB])
        var_eps = sb("var_eps", [P, 2, TB])
        minus_half = sb("minus_half", [P, TB])
        minus_one = sb("minus_one", [P, TB])
        sq_bias = sb("sq_bias", [P, NF])
        eps_c = sb("eps_c", [P, TB])
        pacer = sb("pacer", [P, 1])

        h_turned = ctx.enter_context(nc.psum_tensor("h_turned", [P, 2, TB, DI], F32))
        dA = ctx.enter_context(nc.psum_tensor("dA", [P, DT, T], F32))
        misc = ctx.enter_context(nc.psum_tensor("misc", [P, 2, 2, T], F32))

        s_w_small = sem("small_weights_loaded")
        s_w_ffn = sem("ffn_weights_loaded")
        s_prep = sem("small_weights_scaled")
        s_a = sem("A_exponentiated")
        s_ffn_prep = sem("ffn_weights_scaled")
        s_zero = sem("carry_and_halo_zeroed")
        s_x = [sem(f"x_loaded_{q}") for q in range(NQ)]
        s_res = sem("residual_loaded")
        s_b_saved = sem("B_saved")
        s_rows = [sem(f"B_rows_loaded_{g}") for g in range(NG)]
        s_stored = sem("output_stored")
        s_filled = [sem(f"misc_bank_filled_{b}") for b in (0, 1)]
        s_freed = [sem(f"misc_bank_freed_{b}") for b in (0, 1)]
        s_dA = sem("dA_ready")
        s_dbu = sem("dbu_ready")
        s_scan = sem("scan_done")
        s_turn = sem("h_turned_done")
        s_yadd = sem("y_added")
        s_carry = sem("carry_saved")
        s_xh = sem("xh_ready")
        s_halo = sem("halo_saved")
        s_taps = sem("taps_ready")
        s_pairs = sem("tap_pairs_added")
        s_conv = sem("conv_added")
        s_xth = sem("xc_sigmoid_ready")
        s_xc = sem("xc_ready")
        s_c = sem("C_ready")
        s_exp = sem("softplus_exp_ready")
        s_sq = sem("log1p_squares_ready")
        s_fac = sem("log1p_factors_applied")
        s_delta = sem("delta_ready")
        s_du = sem("du_ready")
        s_zth = sem("z_tanh_ready")
        s_gated = sem("y_gated")
        s_stats = sem("norm_stats")
        s_mv = sem("norm_mean_var")
        s_rstd = sem("norm_rstd_steps")
        s_norm = sem("norm_applied")
        s_gth = sem("gate_tanh_ready")
        s_hid = sem("hidden_ready")

        block = ctx.enter_context(nc.Block())

        def filled(eng, job):
            eng.wait_ge(s_filled[job.bank], job.before + 1)

        def freed(eng, job):
            eng.wait_ge(s_freed[job.bank], job.before + 1)

        def bank_free_for(eng, job):
            if not (isinstance(job.before, int) and job.before == 0):
                eng.wait_ge(s_freed[job.bank], job.before)

        def over_chunks(eng, step):
            step(-1)
            step(0)
            step(1)
            with eng.Fori(2, CH - 1) as c:
                step(c)
            step(CH - 1)
            step(CH)

        def early(c, n):
            return isinstance(c, int) and c < n

        @block.sync
        def _(sp):
            small = [
                (in_w, in_wT, "(k p) e -> p k e"), (xproj_w, xproj_wT, "(k p) e -> p k e"),
                (out_w, out_wT, "(k p) e -> p k e"), (conv_ws, conv_w, "(k p) e -> p k e"),
                (a_neg, A_log, "(k p) e -> p k e"),
            ]
            for q in range(NQ):
                if q == 0:
                    sp.dma_start(x_in[:, q, :, :], xT[q, :, 0:T].rearrange("(k p) t -> p k t", p=P)).then_inc(s_x[q], 16)
                for dst, src, how in small:
                    sp.dma_start(dst[:, q, :, :], src[q].rearrange(how, p=P)).then_inc(s_w_small, 16)
                sp.dma_start(dt_w[:, q, :], dt_wT[q]).then_inc(s_w_small, 16)
                for dst, src in ((conv_bs, conv_b), (dt_bs, dt_b), (d_skip, Dp)):
                    sp.dma_start(dst[:, q, :], src[q]).then_inc(s_w_small, 16)
            sp.dma_start(ident[:, :], ident_in).then_inc(s_w_small, 16)
            sp.dma_start(res[:, :, :], x[0:T, :].rearrange("(b p) f -> p b f", p=P)).then_inc(s_res, 16)
            sp.dma_start(gate_w[:, :, :].bitcast(I32), w_gateT.rearrange("(k p) e -> p k e", p=P)).then_inc(s_w_ffn, 16)
            sp.dma_start(up_w[:, :, :].bitcast(I32), w_upT.rearrange("(k p) e -> p k e", p=P)).then_inc(s_w_ffn, 16)
            sp.dma_start(down_w[:, :, :].bitcast(I32), w_downT.rearrange("(k p) e -> p k e", p=P)).then_inc(s_w_ffn, 16)

            def save_b(c, q):
                u = 2 * c + q
                freed(sp, MiscJob(c - 1 + q, 1 - q, "P", CH))
                if not early(c, 1):
                    sp.wait_ge(s_dbu, (u - 2) * NS + NS)
                sp.dma_start(b_scratch[q], dt_sb[R:R + NS, :]).then_inc(s_b_saved, 16)
                sp.wait_ge(s_b_saved, (u + 1) * 16)

            def load_rows(c, q, g):
                u = 2 * c + q
                if g >= NG or not (early(c, 1) and q == 0):
                    sp.wait_ge(s_dbu, u * NS + (g - NG) * SG + SG)
                rows = b_scratch[q, g * SG:(g + 1) * SG, :].partition_broadcast(P)
                sp.dma_start(b_rows[:, g % NG, :, :], rows).then_inc(s_rows[g % NG], 16)

            def half(c, q):
                parts = parts_of(2 if not isinstance(c, int) else c, q, CH)
                u = 2 * c + q
                if "scan" in parts:
                    load_rows(c, q, 4)
                if q == 0 and not early(c, 2):
                    sp.wait_ge(s_norm, (2 * (c - 2) + 2) * TB)
                    sp.dma_start(out[bass.ds((c - 2) * T, T), :].rearrange("(b p) f -> p b f", p=P),
                                 xn[:, :, :]).then_inc(s_stored, 16)
                if "scan" in parts:
                    load_rows(c, q, 5)
                    load_rows(c, q, 6)
                    if q == 0 and not early(c, 1):
                        sp.wait_ge(s_norm, (2 * (c - 1) + 1) * TB)
                        sp.dma_start(res[:, :, :],
                                     x[bass.ds(c * T, T), :].rearrange("(b p) f -> p b f", p=P)).then_inc(s_res, 16)
                    load_rows(c, q, 7)
                if "front" in parts:
                    nxt = (c, 1) if q == 0 else (c + 1, 0)
                    save_b(*nxt)
                    load_rows(*nxt, 0)
                    load_rows(*nxt, 1)
                    load_rows(*nxt, 2)
                    if not (isinstance(c, int) and c == CH - 1):
                        sp.wait_ge(s_fac, NF * 2 * (u + 2))
                        sp.dma_start(x_in[:, q, :, :],
                                     xT[q, :, bass.ds((c + 1) * T, T)].rearrange("(k p) t -> p k t", p=P)
                                     ).then_inc(s_x[q], 16)
                    load_rows(*nxt, 3)

            def step(c):
                for q in (0, 1):
                    half(c, q)

            over_chunks(sp, step)
            sp.wait_ge(s_norm, 2 * CH * TB)
            sp.dma_start(out[(CH - 1) * T:, :].rearrange("(b p) f -> p b f", p=P), xn[:, :, :]).then_inc(s_stored, 16)
            sp.wait_ge(s_stored, 16 * CH)

        @block.tensor
        def _(pe):
            pe.wait_ge(s_prep, 1)
            pe.wait_ge(s_w_small, 16 * (2 * 9 + 1))

            def mm(out_, lhsT, rhs, k, n):
                return nc.tensor.matmul(out_, lhsT, rhs, start=(k == 0), stop=(k == n - 1), skip_group_check=True)

            def turn(c, q, s, d):
                u = 2 * c + q
                i = u * NS + s
                pe.wait_ge(s_scan, i * DT + d + 1)
                if d == 0 and not (early(c, 1) and q == 0 and s < 2):
                    pe.wait_ge(s_yadd, i - 1)
                for b in range(TB):
                    last = nc.tensor.transpose(h_turned[:, s % 2, b, d * P:(d + 1) * P],
                                               h[:, s % 2, d, b * P:(b + 1) * P], ident[:, :])
                last.then_inc(s_turn, 1)

            def half(c, hh):
                kc = 2 if not isinstance(c, int) else c
                parts = parts_of(kc, hh, CH)
                u = 2 * c + hh
                qf, qn = 1 - hh, 1 - hh
                un = u + 1

                def job(name):
                    j = MiscJob(c, hh, name, CH)
                    bank_free_for(pe, j)
                    return j

                def y_back(j2):
                    j = job(f"Y{j2}")
                    pe.wait_ge(s_yadd, u * NS)
                    for i in range(2):
                        for b in range(TB):
                            d = 2 * j2 + i
                            last = nc.tensor.transpose(misc[:, j.bank, i, b * P:(b + 1) * P],
                                                       y_t[:, qf, b, d * P:(d + 1) * P], ident[:, :])
                    last.then_inc(s_filled[j.bank], 1)

                def project_in(j2, name, q, first, cc):
                    j = job(f"{name}{j2}")
                    pe.wait_ge(s_x[q], 16 * (cc + 1))
                    for i in range(2):
                        e = first + (2 * j2 + i) * P
                        for k in range(KM):
                            last = mm(misc[:, j.bank, i, :], in_w[:, q, k, e:e + P], x_in[:, q, k, :], k, KM)
                    last.then_inc(s_filled[j.bank], 1)

                def project_out():
                    j = job("O")
                    pe.wait_ge(s_gated, u)
                    for b in range(TB):
                        for k in range(DT):
                            last = mm(misc[:, j.bank, b, :], zs[:, k, b * P:(b + 1) * P], out_w[:, qf, k, :], k, DT)
                    last.then_inc(s_filled[j.bank], 1)

                def xproj():
                    j = job("P")
                    pe.wait_ge(s_xc, 2 * un + 2)
                    for k in range(DT):
                        mm(misc[0:R + NS, j.bank, 0, :], xproj_w[:, qn, k, 0:R + NS], xc[:, qn, k, :], k, DT)
                    for b in range(TB):
                        for k in range(DT):
                            last = mm(misc[:, j.bank, 1, b * NS:(b + 1) * NS], xc[:, qn, k, b * P:(b + 1) * P],
                                      xproj_w[:, qn, k, R + NS:R + 2 * NS], k, DT)
                    last.then_inc(s_filled[j.bank], 1)

                def dt_proj(j2):
                    j = job(f"D{j2}")
                    freed(pe, MiscJob(c, hh, "P", CH))
                    for i in range(2):
                        e = (2 * j2 + i) * P
                        last = mm(misc[:, j.bank, i, :], dt_w[:, qn, e:e + P], dt_sb[0:R, :], 0, 1)
                    last.then_inc(s_filled[j.bank], 1)

                def turn_norm(j2):
                    j = job(f"T{j2}")
                    pe.wait_ge(s_norm, (2 * (c - 1) + 1) * TB)
                    for i in range(2):
                        for b in range(TB):
                            k = 2 * j2 + i
                            last = nc.tensor.transpose(misc[:, j.bank, i, b * P:(b + 1) * P],
                                                       xn[:, b, k * P:(k + 1) * P], ident[:, :])
                    last.then_inc(s_filled[j.bank], 1)

                def gate_up(f):
                    j = job(f"G{f}")
                    if f == 0:
                        freed(pe, MiscJob(c, 0, "T1", CH))
                        pe.wait_ge(s_ffn_prep, 3)
                    for i, w in enumerate((gate_w, up_w)):
                        for k in range(KD):
                            last = mm(misc[:, j.bank, i, :], w[:, k, f * P:(f + 1) * P], xnT[:, k, :], k, KD)
                    last.then_inc(s_filled[j.bank], 1)

                def down(b, third):
                    j = MiscJob(c, hh, f"W{b}", CH)
                    if third == 0:
                        bank_free_for(pe, j)
                    for f in range(4 * third, 4 * third + 4):
                        if b == 0:
                            pe.wait_ge(s_hid, FT * (c - 1) + f + 1)
                        last = mm(misc[:, j.bank, :, :], hid[:, f, b * P:(b + 1) * P], down_w[:, f, :], f, FT)
                    if third == 2:
                        last.then_inc(s_filled[j.bank], 1)

                for s in range(NS):
                    if "scan" in parts:
                        turn(c, hh, s, 0)
                        turn(c, hh, s, 1)
                    if "fin" in parts:
                        if s == 0:
                            y_back(0)
                            y_back(1)
                        if s == 3:
                            project_out()
                    if "front" in parts:
                        if s in (1, 2):
                            project_in(s - 1, "X", qn, 0, c if hh == 0 else c + 1)
                    if "ffn" in parts and hh == 1 and s == 2:
                        gate_up(7)
                    if "scan" in parts and s in (4, 5):
                        project_in(s - 4, "Z", hh, DI, c)
                    if "ffn" in parts and hh == 0 and s == 7:
                        turn_norm(0)
                        turn_norm(1)
                    if "ffn" in parts and hh == 1 and s in (5, 6, 7, 8):
                        gate_up(s + 3)
                    if "front" in parts and s == 8:
                        xproj()
                    if "front" in parts and s == 11:
                        dt_proj(1)
                    if "ffn" in parts and hh == 0 and s in (9, 10, 11):
                        gate_up(s - 9)
                    if "ffn" in parts and hh == 1 and s in (10, 11):
                        down(0, s - 10)
                    if "front" in parts and s == 9:
                        dt_proj(0)
                    if "ffn" in parts and hh == 0 and s in (12, 13, 14, 15):
                        gate_up(s - 9)
                    if "ffn" in parts and hh == 1 and s >= 12:
                        down((s - 10) // 3, (s - 10) % 3)
                    if "scan" in parts:
                        turn(c, hh, s, 2)
                        turn(c, hh, s, 3)

            def step(c):
                for hh in (0, 1):
                    half(c, hh)

            over_chunks(pe, step)

        @block.scalar
        def _(act):
            act.wait_ge(s_w_small, 16 * (2 * 9 + 1))
            nc.scalar.activation(a_neg[:, :, :, :], a_neg[:, :, :, :], ACT.Exp).then_inc(s_a, 1)

            def half(c, hh):
                kc = 2 if not isinstance(c, int) else c
                parts = parts_of(kc, hh, CH)
                u = 2 * c + hh
                un = u + 1
                qn = 1 - hh

                def exps(s):
                    i = u * NS + s
                    if s == 0:
                        act.wait_ge(s_delta, u + 1)
                    for d in range(DT):
                        if d % 2 == 0 and not (early(c, 1) and hh == 0 and s == 0):
                            act.wait_ge(s_scan, (i - 1) * DT + d + 2)
                        nc.scalar.activation(dA[:, d, :], delta[:, hh, d, :], ACT.Exp,
                                             scale=a_neg[:, hh, d, s:s + 1]).then_inc(s_dA, 1)

                def save_carry(uu, q, s):
                    act.wait_ge(s_scan, (uu * NS + s + 1) * DT)
                    nc.scalar.copy(carry[:, q, s, :], h[:, s % 2, :, T - 1]).then_inc(s_carry, 1)

                def xh_halo():
                    if early(c, 0) or (early(c, 1) and hh == 0):
                        act.wait_ge(s_zero, 5 + NF)
                    else:
                        act.wait_ge(s_halo, un - 1)
                    if not early(c, 0):
                        act.wait_ge(s_delta, un)
                    nc.scalar.copy(xh[:, :, 0:TAPS - 1], halo[:, qn, :, :]).then_inc(s_xh, 1)

                def xh_out(j2):
                    j = MiscJob(c, hh, f"X{j2}", CH)
                    filled(act, j)
                    act.wait_ge(s_xh, un + 1)
                    nc.scalar.copy(xh[:, 2 * j2:2 * j2 + 2, TAPS - 1:], misc[:, j.bank, :, :]).then_inc(s_freed[j.bank], 1)
                    act.wait_ge(s_freed[j.bank], j.before + 1)

                def save_halo():
                    nc.scalar.copy(halo[:, qn, :, :], xh[:, :, T:T + TAPS - 1]).then_inc(s_halo, 1)

                def taps(i):
                    if not (early(c, 0) and i == 0):
                        act.wait_ge(s_conv, 4 * un + i)
                    for k in range(TAPS):
                        last = nc.scalar.activation(tmp4[:, k, :], xh[:, i, k:k + T], ACT.Identity,
                                                    bias=conv_bs[:, qn, i:i + 1] if k == TAPS - 1 else 0.0,
                                                    scale=conv_ws[:, qn, i, k:k + 1])
                    last.then_inc(s_taps, 1)

                def xc_sigmoid(j2):
                    act.wait_ge(s_conv, 4 * un + 2 * j2 + 2)
                    if not (early(c, 0) and j2 == 0):
                        act.wait_ge(s_xc, 2 * un + j2)
                    nc.scalar.activation(th_x[:, :, :], xc[:, qn, 2 * j2:2 * j2 + 2, :], ACT.Tanh).then_inc(s_xth, 1)
                    act.wait_ge(s_xth, 4 * un + 2 * j2 + 1)
                    nc.scalar.activation(th_x[:, :, :], th_x[:, :, :], ACT.Copy, bias=1.0).then_inc(s_xth, 1)

                def dt_b_c_out():
                    j = MiscJob(c, hh, "P", CH)
                    filled(act, j)
                    if not early(c, 0):
                        act.wait_ge(s_b_saved, 16 * un)
                    if not (early(c, 0) or (early(c, 1) and hh == 0)):
                        act.wait_ge(s_yadd, (un - 2) * NS + NS)
                    nc.scalar.copy(c_t[:, qn, :, :], misc[:, j.bank, 1, 0:TB * NS].rearrange("p (b s) -> p b s", s=NS)
                                   ).then_inc(s_c, 1)
                    nc.scalar.copy(dt_sb[:, :], misc[0:R + NS, j.bank, 0, :]).then_inc(s_freed[j.bank], 1)

                def delta_terms(j2):
                    j = MiscJob(c, hh, f"D{j2}", CH)
                    filled(act, j)
                    for i in range(2):
                        d = 2 * j2 + i
                        nc.scalar.activation(tmp4[:, d, :], misc[:, j.bank, i, :], ACT.Abs, bias=dt_bs[:, qn, d:d + 1])
                        last = nc.scalar.activation(delta[:, qn, d, :], misc[:, j.bank, i, :], ACT.Relu,
                                                    bias=dt_bs[:, qn, d:d + 1])
                    last.then_inc(s_freed[j.bank], 1)
                    act.wait_ge(s_freed[j.bank], j.before + 1)
                    u_ = tmp4[:, 2 * j2:2 * j2 + 2, :]
                    nc.scalar.activation(u_, u_, ACT.Exp, scale=-1.0).then_inc(s_exp, 1)

                def square(j2, k):
                    u_ = tmp4[:, 2 * j2:2 * j2 + 2, :]
                    if k == 0:
                        act.wait_ge(s_exp, 2 * un + j2 + 1)
                        if j2 == 1:
                            act.wait_ge(s_fac, NF * (2 * un + 1))
                    if k == 1 and j2 == 0 and "scan" in parts:
                        filled(act, MiscJob(c, hh, "Z1", CH))
                    if k == 2:
                        act.wait_ge(s_fac, NF * (2 * un + j2) + 1)
                    root = LOG1P_LEAD ** 0.5 if k == 0 else 1.0
                    nc.scalar.activation((th_x[:, :, :], x_in[:, hh, :, :], th_x[:, :, :], u_)[k], u_, ACT.Square,
                                         bias=sq_bias[:, k:k + 1], scale=root).then_inc(s_sq, 1)

                def z_tanh(j2):
                    j = MiscJob(c, hh, f"Z{j2}", CH)
                    filled(act, j)
                    if j2 == 0 and "fin" in parts:
                        filled(act, MiscJob(c, hh, "O", CH))
                    nc.scalar.activation(zs[:, 2 * j2:2 * j2 + 2, :], misc[:, j.bank, :, :], ACT.Tanh).then_inc(s_zth, 1)

                def norm_apply(which, cc):
                    n = 2 * cc + which
                    act.wait_ge(s_rstd, 4 * (n + 1))
                    if which == 1:
                        dst, src = xn, xn
                    else:
                        dst, src = xn, res
                    if which == 0 and not early(cc, 1):
                        act.wait_ge(s_stored, 16 * cc)
                    for b in range(TB):
                        nc.scalar.activation(dst[:, b, :], src[:, b, :], ACT.Identity, bias=shift[:, which, b:b + 1],
                                             scale=rstd[:, which, b:b + 1]).then_inc(s_norm, 1)

                def turned_norm_out(j2):
                    j = MiscJob(c, hh, f"T{j2}", CH)
                    filled(act, j)
                    nc.scalar.copy(xnT[:, 2 * j2:2 * j2 + 2, :], misc[:, j.bank, :, :]).then_inc(s_freed[j.bank], 1)

                def gate_out(f):
                    cg, hg = (c, 0) if f <= 6 else (c, 1)
                    j = MiscJob(cg, hg, f"G{f}", CH)
                    filled(act, j)
                    if not (early(c, 2) and f < 2):
                        act.wait_ge(s_hid, FT * (c - 1) + f - 1)
                    nc.scalar.copy(up_f[:, f % 2, :], misc[:, j.bank, 1, :])
                    nc.scalar.activation(th_g[:, f % 2, :], misc[:, j.bank, 0, :], ACT.Tanh).then_inc(s_gth, 1)

                for s in range(NS):
                    if "scan" in parts:
                        exps(s)
                        if s > 0:
                            save_carry(u, hh, s - 1)
                    if s == 0 and "fin" in parts:
                        save_carry(u - 1, qn, NS - 1)
                    if "front" in parts:
                        if s == 2:
                            xh_halo()
                            xh_out(0)
                            taps(0)
                        if s == 3:
                            xh_out(1)
                            save_halo()
                            taps(1)
                        if s == 4:
                            taps(2)
                        if s == 5:
                            xc_sigmoid(0)
                            taps(3)
                        if s == 7:
                            xc_sigmoid(1)
                        if s == 9:
                            dt_b_c_out()
                    if s == 2 and hh == 0 and not early(c, 2):
                        norm_apply(1, c - 2)
                    if "scan" in parts and s in (5, 6):
                        z_tanh(s - 5)
                    if hh == 0 and "ffn" in parts:
                        if s == 6:
                            norm_apply(0, c - 1)
                        if s == 8:
                            turned_norm_out(0)
                            turned_norm_out(1)
                        if s >= 10:
                            gate_out(s - 10)
                    if hh == 1 and "ffn" in parts:
                        if s in (0, 3):
                            gate_out(6 + s // 3)
                        if s in (6, 7, 8, 9):
                            gate_out(s + 2)
                    if "front" in parts:
                        if s in (10, 12):
                            delta_terms(s // 2 - 5)
                            square(s // 2 - 5, 0)
                            square(s // 2 - 5, 1)
                        if s in (11, 13):
                            square(s // 2 - 5, 2)
                            square(s // 2 - 5, 3)

            def step(c):
                for hh in (0, 1):
                    half(c, hh)

            over_chunks(act, step)
            act.wait_ge(s_rstd, 4 * 2 * CH)
            for b in range(TB):
                nc.scalar.activation(xn[:, b, :], xn[:, b, :], ACT.Identity, bias=shift[:, 1, b:b + 1],
                                     scale=rstd[:, 1, b:b + 1]).then_inc(s_norm, 1)

        @block.gpsimd
        def _(pool):
            nc.gpsimd.memset(carry[:, :, :, :], 0.0).then_inc(s_zero, 1)
            nc.gpsimd.memset(halo[:, :, :, :], 0.0).then_inc(s_zero, 1)
            nc.gpsimd.memset(minus_half[:, :], -0.5).then_inc(s_zero, 1)
            nc.gpsimd.memset(minus_one[:, :], -1.0).then_inc(s_zero, 1)
            nc.gpsimd.memset(eps_c[:, :], EPS).then_inc(s_zero, 1)
            for k, (a, _) in enumerate(LOG1P_FACTORS):
                root = LOG1P_LEAD ** 0.5 if k == 0 else 1.0
                nc.gpsimd.memset(sq_bias[:, k:k + 1], root * a).then_inc(s_zero, 1)
            pool.wait_ge(s_zero, 5 + NF)

            def rstd_steps(n):
                w = n[1]
                k = 2 * n[0] + w
                pool.wait_ge(s_mv, k + 1)
                if not (early(n[0], 1)):
                    pool.wait_ge(s_norm, (k - 2 + 1) * TB)
                nc.gpsimd.tensor_tensor(var_eps[:, w, :], mv[:, w, :, 1], eps_c[:, :], ALU.add).then_inc(s_rstd, 1)
                nc.gpsimd.tensor_tensor(negm[:, w, :], mv[:, w, :, 0], minus_one[:, :], ALU.mult).then_inc(s_rstd, 1)
                pool.wait_ge(s_rstd, 4 * k + 2)
                nc.gpsimd.tensor_tensor(rstd[:, w, :], var_eps[:, w, :], minus_half[:, :], ALU.pow).then_inc(s_rstd, 1)
                pool.wait_ge(s_rstd, 4 * k + 3)
                nc.gpsimd.tensor_tensor(shift[:, w, :], negm[:, w, :], rstd[:, w, :], ALU.mult).then_inc(s_rstd, 1)

            def half(c, hh):
                kc = 2 if not isinstance(c, int) else c
                parts = parts_of(kc, hh, CH)
                u = 2 * c + hh
                un = u + 1
                qn = 1 - hh

                def dbu_of(s):
                    i = u * NS + s
                    g = s // SG
                    if s == 0:
                        pool.wait_ge(s_du, u + 1)
                    if s % SG == 0:
                        pool.wait_ge(s_rows[g % NG], 16 * (GROUPS // NG * u + g // NG + 1))
                    if not (early(c, 1) and hh == 0 and s < 2):
                        pool.wait_ge(s_scan, (i - 1) * DT)
                    rows = b_rows[:, g % NG, s % SG, :].unsqueeze(1).broadcast_to([P, DT, T])
                    nc.gpsimd.tensor_tensor(dbu[:, s % 2, :, :], du[:, hh, :, :], rows, ALU.mult).then_inc(s_dbu, 1)

                def gate_y():
                    freed(pool, MiscJob(c, hh, "Y1", CH))
                    nc.gpsimd.tensor_tensor(zs[:, :, :], zs[:, :, :], xc[:, qn, :, :], ALU.mult).then_inc(s_gated, 1)

                def conv_add(i):
                    n = 4 * un + i
                    pool.wait_ge(s_taps, n + 1)
                    if i == 0 and "fin" in parts:
                        pool.wait_ge(s_gated, u)
                    nc.gpsimd.tensor_tensor(tmp4[:, 0:2, :], tmp4[:, 0:2, :], tmp4[:, 2:4, :], ALU.add).then_inc(s_pairs, 1)
                    pool.wait_ge(s_pairs, n + 1)
                    nc.gpsimd.tensor_tensor(xc[:, qn, i, :], tmp4[:, 0, :], tmp4[:, 1, :], ALU.add).then_inc(s_conv, 1)

                def xc_silu(j2):
                    pool.wait_ge(s_xth, 4 * un + 2 * j2 + 2)
                    nc.gpsimd.tensor_tensor(xc[:, qn, 2 * j2:2 * j2 + 2, :], xc[:, qn, 2 * j2:2 * j2 + 2, :],
                                            th_x[:, :, :], ALU.mult).then_inc(s_xc, 1)

                def delta_sum():
                    pool.wait_ge(s_fac, NF * (2 * un + 2))
                    nc.gpsimd.tensor_tensor(delta[:, qn, :, :], delta[:, qn, :, :], xh[:, :, 0:T], ALU.add).then_inc(s_delta, 1)

                def du_of():
                    pool.wait_ge(s_delta, un + 1)
                    pool.wait_ge(s_xc, 2 * un + 2)
                    nc.gpsimd.tensor_tensor(du[:, qn, :, :], delta[:, qn, :, :], xc[:, qn, :, :], ALU.mult).then_inc(s_du, 1)

                def hidden(f, cc, hf):
                    freed(pool, MiscJob(cc, hf, f"G{f}", CH))
                    nc.gpsimd.tensor_tensor(hid[:, f, :], th_g[:, f % 2, :], up_f[:, f % 2, :], ALU.mult).then_inc(s_hid, 1)

                for s in range(NS):
                    if "scan" in parts:
                        dbu_of(s)
                    if s == 1 and hh == 0 and not early(c, 2):
                        rstd_steps((c - 2, 1))
                    if "fin" in parts and s == 1:
                        gate_y()
                    if hh == 1 and "ffn" in parts:
                        if s in (0, 1):
                            hidden(s + 5, c, 0)
                        if s == 4:
                            hidden(7, c, 1)
                        if s in (7, 8, 9, 10):
                            hidden(s + 1, c, 1)
                    if "front" in parts:
                        if s in (3, 4):
                            conv_add(s - 3)
                        if s == 5:
                            conv_add(2)
                        if s == 6:
                            xc_silu(0)
                            conv_add(3)
                        if s == 7:
                            xc_silu(1)
                    if hh == 0 and "ffn" in parts:
                        if s == 5:
                            rstd_steps((c - 1, 0))
                        if s >= 11:
                            hidden(s - 11, c, 0)
                    if "front" in parts:
                        if s == 14:
                            delta_sum()
                            du_of()

            def step(c):
                for hh in (0, 1):
                    half(c, hh)

            over_chunks(pool, step)
            rstd_steps((CH - 1, 1))

        @block.vector
        def _(dve):
            dve.wait_ge(s_w_small, 16 * (2 * 9 + 1))
            nc.vector.tensor_scalar(in_w[:, :, :, DI:], in_w[:, :, :, DI:], 0.5, None, ALU.mult)
            nc.vector.tensor_scalar(conv_ws[:, :, :, :], conv_ws[:, :, :, :], 0.5, None, ALU.mult)
            nc.vector.tensor_scalar(conv_bs[:, :, :], conv_bs[:, :, :], 0.5, None, ALU.mult)
            dve.wait_ge(s_a, 1)
            nc.vector.tensor_scalar(a_neg[:, :, :, :], a_neg[:, :, :, :], -1.0, None, ALU.mult).then_inc(s_prep, 1)
            dve.wait_ge(s_zero, 2)

            def norm_stats(which, cc, src, job):
                k = 2 * cc + which
                freed(dve, job)
                for b in range(TB):
                    nc.vector.bn_stats(stats[:, which, b, :], src[:, b, :]).then_inc(s_stats, 1)
                dve.wait_ge(s_stats, TB * (k + 1))
                if not early(cc, 1):
                    dve.wait_ge(s_rstd, 4 * (k - 2 + 1))
                nc.vector.tensor_copy(pacer[:, :], stats[:, which, 0, 0:1])
                for b in range(TB):
                    last = nc.vector.bn_aggr(mv[:, which, b, :], stats[:, which, b, :])
                last.then_inc(s_mv, 1)

            def down_out(c, hh, b):
                j = MiscJob(c, hh, f"W{b}", CH)
                filled(dve, j)
                nc.vector.tensor_tensor(xn[:, b, :], misc[:, j.bank, :, :].rearrange("p a t -> p (a t)"),
                                        xn[:, b, :], ALU.add).then_inc(s_freed[j.bank], 1)

            def half(c, hh):
                kc = 2 if not isinstance(c, int) else c
                parts = parts_of(kc, hh, CH)
                u = 2 * c + hh
                qn = 1 - hh

                def scan(s, d):
                    i = u * NS + s
                    if d % 2 == 0:
                        dve.wait_ge(s_dA, i * DT + d + 2)
                    if d == 0:
                        dve.wait_ge(s_dbu, i + 1)
                        if not (early(c, 1) and hh == 0 and s < 2):
                            dve.wait_ge(s_carry, i - 1)
                    if not (early(c, 1) and hh == 0 and s < 2):
                        dve.wait_ge(s_turn, (i - 2) * DT + d + 1)
                    nc.vector.tensor_tensor_scan(h[:, s % 2, d, :], dA[:, d, :], dbu[:, s % 2, d, :],
                                                 carry[:, hh, s, d:d + 1], ALU.mult, ALU.add).then_inc(s_scan, 1)

                def add_y(uu, q, s, cc):
                    i = uu * NS + s
                    dve.wait_ge(s_turn, (i + 1) * DT)
                    if s == 0:
                        dve.wait_ge(s_c, uu + 1)
                    else:
                        dve.wait_ge(s_yadd, i)
                    for b in range(TB):
                        if s == 0:
                            last = nc.vector.tensor_scalar(y_t[:, q, b, :], h_turned[:, s % 2, b, :],
                                                           c_t[:, q, b, s:s + 1], None, ALU.mult)
                        else:
                            last = nc.vector.scalar_tensor_tensor(y_t[:, q, b, :], h_turned[:, s % 2, b, :],
                                                                  c_t[:, q, b, s:s + 1], y_t[:, q, b, :],
                                                                  ALU.mult, ALU.add)
                    last.then_inc(s_yadd, 1)

                def y_skip(j2):
                    j = MiscJob(c, hh, f"Y{j2}", CH)
                    filled(dve, j)
                    for i in range(2):
                        d = 2 * j2 + i
                        last = nc.vector.scalar_tensor_tensor(xc[:, qn, d, :], xc[:, qn, d, :], d_skip[:, qn, d:d + 1],
                                                              misc[:, j.bank, i, :], ALU.mult, ALU.add)
                    last.then_inc(s_freed[j.bank], 1)

                def residual():
                    j = MiscJob(c, hh, "O", CH)
                    filled(dve, j)
                    cf = c - 1 if hh == 0 else c
                    dve.wait_ge(s_res, 16 * (cf + 1))
                    part = res[:, :, qn * DM:(qn + 1) * DM]
                    nc.vector.tensor_tensor(part, misc[:, j.bank, :, :], part, ALU.add).then_inc(s_freed[j.bank], 1)

                def z_silu(j2):
                    j = MiscJob(c, hh, f"Z{j2}", CH)
                    dve.wait_ge(s_zth, 2 * u + j2 + 1)
                    nc.vector.scalar_tensor_tensor(zs[:, 2 * j2:2 * j2 + 2, :], zs[:, 2 * j2:2 * j2 + 2, :], 1.0,
                                                   misc[:, j.bank, :, :], ALU.add, ALU.mult).then_inc(s_freed[j.bank], 1)

                def gate_silu(f):
                    j = MiscJob(c, 0 if f <= 6 else 1, f"G{f}", CH)
                    dve.wait_ge(s_gth, FT * (c - 1) + f + 1)
                    nc.vector.scalar_tensor_tensor(th_g[:, f % 2, :], th_g[:, f % 2, :], 1.0,
                                                   misc[:, j.bank, 0, :], ALU.add, ALU.mult).then_inc(s_freed[j.bank], 1)

                def factor(j2, k):
                    un = u + 1
                    n = NF * (2 * un + j2) + k
                    dve.wait_ge(s_sq, n + 1)
                    if k > 0:
                        dve.wait_ge(s_fac, n)
                    if k == 0 and j2 == 0:
                        dve.wait_ge(s_halo, un + 1)
                        dve.wait_ge(s_taps, 4 * (un + 1))
                    u_ = tmp4[:, 2 * j2:2 * j2 + 2, :]
                    acc = xh[:, 2 * j2:2 * j2 + 2, 0:T]
                    b_ = LOG1P_FACTORS[k][1] * (LOG1P_LEAD if k == 0 else 1.0)
                    nc.vector.scalar_tensor_tensor(acc, (th_x[:, :, :], x_in[:, hh, :, :], th_x[:, :, :], u_)[k], b_,
                                                   u_ if k == 0 else acc, ALU.add, ALU.mult).then_inc(s_fac, 1)

                for s in range(NS):
                    if "scan" in parts:
                        scan(s, 0)
                        scan(s, 1)
                    if s > 0 and "scan" in parts:
                        add_y(u, hh, s - 1, c)
                    if s == 0 and "fin" in parts:
                        add_y(u - 1, qn, NS - 1, c)
                    if "ffn" in parts and hh == 0 and s >= 10:
                        gate_silu(s - 10)
                    if "ffn" in parts and hh == 1:
                        if s in (0, 3):
                            gate_silu(6 + s // 3)
                        if s in (6, 7, 8, 9):
                            gate_silu(s + 2)
                    if s == 0 and hh == 0 and not early(c, 2):
                        down_out(c - 1, 1, 1)
                    if "scan" in parts:
                        scan(s, 2)
                        scan(s, 3)
                    if s == 0 and hh == 0 and not early(c, 2):
                        norm_stats(1, c - 2, xn, MiscJob(c - 1, 1, "W1", CH))
                    if "fin" in parts:
                        if s == 1:
                            y_skip(0)
                            y_skip(1)
                        if s == 4:
                            residual()
                            if hh == 0:
                                norm_stats(0, c - 1, res, MiscJob(c, 0, "O", CH))
                    if "scan" in parts and s in (5, 6):
                        z_silu(s - 5)
                    if "ffn" in parts and hh == 1:
                        if s == 13:
                            down_out(c, 1, 0)
                    if "front" in parts and s in (10, 11, 12, 13):
                        factor(s // 2 - 5, 2 * (s % 2))
                        factor(s // 2 - 5, 2 * (s % 2) + 1)
                if isinstance(c, int) and c == 0 and hh == 1:
                    dve.wait_ge(s_w_ffn, 48)
                    for w, scale in ((gate_w, 0.5 * WEIGHT_SCALE), (up_w, WEIGHT_SCALE), (down_w, WEIGHT_SCALE)):
                        nc.vector.tensor_scalar(w[:, :, :], w[:, :, :].bitcast(I32), scale, None, ALU.mult
                                                ).then_inc(s_ffn_prep, 1)

            def step(c):
                for hh in (0, 1):
                    half(c, hh)

            over_chunks(dve, step)
            down_out(CH, 1, 1)
            norm_stats(1, CH - 1, xn, MiscJob(CH, 1, "W1", CH))


def kernel(**inputs):
    import numpy as np
    import concourse.bacc as bacc
    from concourse.bass_utils import run_bass_kernel_spmd

    get = {name.replace("L0_attn_", "").replace("L0_ffn_", ""): np.asarray(a) for name, a in inputs.items()}
    x = get["x"][0]
    dm = x.shape[1] // 2

    def both(name, turn=False):
        return np.stack([get[name + t].T if turn else get[name + t] for t in "12"])

    def per_channel(name):
        return both(name).reshape(2, -1, P).transpose(0, 2, 1)

    arrays = {
        "xT": np.stack([x[:, :dm].T, x[::-1, dm:].T]),
        "x": x,
        "in_wT": both("in_w", True), "conv_w": both("conv_w"), "conv_b": per_channel("conv_b"),
        "xproj_wT": both("xproj_w", True), "dt_wT": both("dt_w", True), "dt_b": per_channel("dt_b"),
        "A_log": both("A_log"), "Dp": per_channel("D"), "out_wT": both("out_w", True),
        "w_gateT": get["w_gate"].T, "w_upT": get["w_up"].T, "w_downT": get["w_down"].T,
        "ident_in": np.eye(P, dtype=np.float32),
    }
    nc = bacc.Bacc("TRN2", target_bir_lowering=False, num_devices=1)
    feeds, args = {}, []
    for name, a in arrays.items():
        a = np.ascontiguousarray(a)
        feeds[f"{name}_dram"] = a
        args.append(nc.dram_tensor(f"{name}_dram", a.shape, mybir.dt.from_np(a.dtype), kind="ExternalInput").ap())
    out = nc.dram_tensor("out_dram", x.shape, F32, kind="ExternalOutput").ap()
    mamba_pair_ffn_kernel(nc, *args, out)
    r = run_bass_kernel_spmd(nc, [feeds], core_ids=[0])
    return r.results[0]["out_dram"].reshape(1, *x.shape)
```

```python
from contextlib import ExitStack

import concourse.bass as bass
from concourse import mybir

ALU = mybir.AluOpType
ACT = mybir.ActivationFunctionType
F32 = mybir.dt.float32
I32 = mybir.dt.int32

P = 128
T = 256
TB = T // P
NS = 16
NQ = 2
TAPS = 4
EPS = 1e-5
WEIGHT_SCALE = 1.0 / 127.0

LOG1P_LEAD = 0.005232691452828611
LOG1P_FACTORS = [(-2.3216866366639644, 0.43240686292846314), (-1.4247358216099517, 2.702103630824708),
                 (1.009357722539173, 1.1060623827831724), (-0.08225184120489804, 3.257468775834742)]
NF = len(LOG1P_FACTORS)

MISC = 3
JOBS = {
    0: [("O", "fin"), ("Z0", "scan"), ("Z1", "scan"), ("P", "front"), ("T0", "ffn"), ("T1", "ffn"),
        ("D0", "front"), ("D1", "front"), ("G0", "ffn"), ("G1", "ffn"), ("G2", "ffn"), ("G3", "ffn"),
        ("X0", "ahead"), ("G4", "ffn"), ("X1", "ahead"), ("G5", "ffn")],
    1: [("G6", "ffn"), ("G7", "ffn"), ("G8", "ffn"), ("G9", "ffn"), ("O", "fin"), ("Z0", "scan"), ("Z1", "scan"),
        ("P", "front"), ("G10", "ffn"), ("G11", "ffn"), ("D0", "front"), ("D1", "front"), ("W0", "ffn"),
        ("W1", "ffn"), ("X0", "ahead"), ("X1", "ahead")],
}
BANK = {(h, name): (i + h * len(JOBS[0])) % MISC for h in (0, 1) for i, (name, _) in enumerate(JOBS[h])}


def ring(n, slots):
    short = next(k for k in range(slots) if (n - k * (slots - 1)) % slots == 0)
    full = n - short * (slots - 1)
    return [i % slots if i < full else (i - full) % (slots - 1) for i in range(n)]


def uses_back(slots, at):
    return next(n for n in range(1, len(slots)) if slots[at - n] == slots[at])


SLOTS = 5
SLOT = ring(NQ * NS, SLOTS)
ADDED = {0: (), 1: (1, 3, 5, 7, 9, 11, 13, 15)}
PAIR_BANKS = 3
PAIR_BANK = ring(2 * NQ * NS, PAIR_BANKS)


def parts_of(c, h, chunks):
    if c < 0:
        return {"front", "ahead"} if h == 1 else {"ahead"}
    if c >= chunks:
        return {0: {"fin", "ffn"}, 1: {"ffn"}}[h]
    parts = {"scan"}
    if c > 0 or h == 1:
        parts.add("fin")
    if c > 0:
        parts.add("ffn")
    if c < chunks - 1 or h == 0:
        parts.add("front")
    if c < chunks - 1:
        parts.add("ahead")
    return parts


def jobs_of(c, h, chunks):
    return [(name, BANK[h, name]) for name, part in JOBS[h] if part in parts_of(c, h, chunks)]


def used_before(c, bank, chunks):
    known = c if isinstance(c, int) else 2
    n = sum(b == bank for k in range(-1, known) for h in (0, 1) for _, b in jobs_of(k, h, chunks))
    if isinstance(c, int):
        return n
    per_step = sum(b == bank for h in (0, 1) for _, b in jobs_of(2, h, chunks))
    return (c - 2) * per_step + n


def added_before(c, q, s, back=0):
    per_step = len(ADDED[0]) + len(ADDED[1])
    return c * per_step + (q * len(ADDED[0]) + sum(b < s for b in ADDED[q]) - back * per_step)


def sums_before(c, q, s, back=0):
    a = s - 1 if s in ADDED[q] else s
    per_step = 2 * NS - len(ADDED[0]) - len(ADDED[1])
    return c * per_step + (q * NS + a - added_before(0, q, a) - back * per_step)


class MiscJob:

    def __init__(self, c, h, name, chunks):
        sort_c = c if isinstance(c, int) else 2
        listed = [(k, n, b) for k in (0, 1) for n, b in jobs_of(sort_c, k, chunks)]
        at = [(k, n) for k, n, _ in listed].index((h, name))
        self.bank = listed[at][2]
        self.before = used_before(c, self.bank, chunks) + sum(b == self.bank for _, _, b in listed[:at])


def mamba_pair_ffn_kernel(nc, xT, x, in_wT, conv_w, conv_b, xproj_wT, dt_wT, dt_b, A_log, Dp, out_wT,
                          w_gateT, w_upT, w_downT, ident_in, out):
    L, DIM = x.shape
    DM = DIM // NQ
    KM = DM // P
    DI = in_wT[0].shape[1] // 2
    DT = DI // P
    R = dt_wT[0].shape[0]
    KD = DIM // P
    HID = w_gateT.shape[1]
    FT = HID // P
    CH = L // T
    NG = 4
    assert L % T == 0 and CH >= 5 and DT == 4 and KM == 2 and TB == 2 and FT == 12 and KD == 4

    bc_scratch = nc.dram_tensor("bc_scratch", [NQ, 2 * NS, T], F32).ap()

    with ExitStack() as ctx:
        def sb(name, shape, dt=F32):
            return ctx.enter_context(nc.sbuf_tensor(name, shape, dt))

        def sem(name):
            return ctx.enter_context(nc.semaphore(name))

        in_w = sb("in_w", [P, NQ, KM, 2 * DI])
        xproj_w = sb("xproj_w", [P, NQ, DT, R + 2 * NS])
        dt_w = sb("dt_w", [R, NQ, DI])
        out_w = sb("out_w", [P, NQ, DT, DM])
        gate_w = sb("gate_w", [P, KD, HID])
        up_w = sb("up_w", [P, KD, HID])
        down_w = sb("down_w", [P, FT, DIM])
        ident = sb("ident", [P, P])
        conv_ws = sb("conv_ws", [P, NQ, DT, TAPS])
        conv_bs = sb("conv_bs", [P, NQ, DT])
        dt_bs = sb("dt_bs", [P, NQ, DT])
        a_neg = sb("a_neg", [P, NQ, DT, NS])
        d_skip = sb("d_skip", [P, NQ, DT])
        b_rows = sb("b_rows", [P, NG, T])
        c_rows = sb("c_rows", [P, NG, T])
        states = sb("states", [P, SLOTS, DT, T])
        carry = sb("carry", [P, NQ, NS, DT])
        delta = sb("delta", [P, NQ, DT, T])
        du = sb("du", [P, NQ, DT, T])
        xc = sb("xc", [P, NQ, DT, T])
        x_in = sb("x_in", [P, NQ, KM, T])
        xh = sb("xh", [P, DT, TAPS - 1 + T])
        halo = sb("halo", [P, NQ, DT, TAPS - 1])
        tmp4 = sb("tmp4", [P, 4, T])
        th_x = sb("th_x", [P, 2, T])
        sq_2 = sb("sq_2", [P, 2, T])
        dt_sb = sb("dt_sb", [R + 2 * NS, T])
        zs = sb("zs", [P, DT, T])
        res = sb("res", [P, TB, DIM])
        xn = sb("xn", [P, TB, DIM])
        xnT = sb("xnT", [P, KD, T])
        th_g = sb("th_g", [P, 2, T])
        up_f = sb("up_f", [P, 2, T])
        hid = sb("hid", [P, FT, T])
        stats = sb("stats", [P, 2, TB, 6])
        mv = sb("mv", [P, 2, TB, 2])
        rstd = sb("rstd", [P, 2, TB])
        negm = sb("negm", [P, 2, TB])
        shift = sb("shift", [P, 2, TB])
        var_eps = sb("var_eps", [P, 2, TB])
        minus_half = sb("minus_half", [P, TB])
        minus_one = sb("minus_one", [P, TB])
        sq_bias = sb("sq_bias", [P, NF])
        eps_c = sb("eps_c", [P, TB])
        pacer = sb("pacer", [P, 1])

        dA = ctx.enter_context(nc.psum_tensor("dA", [P, PAIR_BANKS, 2, T], F32))
        y = ctx.enter_context(nc.psum_tensor("y", [P, DT, T], F32))
        misc = ctx.enter_context(nc.psum_tensor("misc", [P, MISC, 2, T], F32))

        s_w_small = sem("small_weights_loaded")
        s_w_ffn = sem("ffn_weights_loaded")
        s_prep = sem("small_weights_scaled")
        s_a = sem("A_exponentiated")
        s_ffn_prep = sem("ffn_weights_scaled")
        s_zero = sem("carry_and_halo_zeroed")
        s_x = [sem(f"x_loaded_{q}") for q in range(NQ)]
        s_res = sem("residual_loaded")
        s_bc_saved = sem("B_and_C_saved")
        s_b_row = [sem(f"B_row_loaded_{g}") for g in range(NG)]
        s_c_row = [sem(f"C_row_loaded_{g}") for g in range(NG)]
        s_stored = sem("output_stored")
        s_filled = [sem(f"misc_bank_filled_{b}") for b in range(MISC)]
        s_freed = [sem(f"misc_bank_freed_{b}") for b in range(MISC)]
        s_dA = sem("dA_ready")
        s_dbu = sem("dbu_ready")
        s_scan = sem("scan_done")
        s_prod = sem("C_times_h_done")
        s_add = sem("pair_of_C_times_h_added")
        s_sum = sem("y_summed")
        s_skip = sem("y_with_skip_ready")
        s_carry = sem("carry_saved")
        s_xh = sem("xh_ready")
        s_halo = sem("halo_saved")
        s_taps = sem("taps_ready")
        s_pairs = sem("tap_pairs_added")
        s_conv = sem("conv_added")
        s_xth = sem("xc_tanh_ready")
        s_xc = sem("xc_ready")
        s_exp = sem("softplus_exp_ready")
        s_sq = sem("log1p_squares_ready")
        s_fac = sem("log1p_factors_applied")
        s_delta = sem("delta_ready")
        s_du = sem("du_ready")
        s_zth = sem("z_tanh_ready")
        s_gated = sem("y_gated")
        s_stats = sem("norm_stats")
        s_mv = sem("norm_mean_var")
        s_rstd = sem("norm_rstd_steps")
        s_norm = sem("norm_applied")
        s_gth = sem("gate_tanh_ready")
        s_hid = sem("hidden_ready")

        block = ctx.enter_context(nc.Block())

        def filled(eng, job):
            eng.wait_ge(s_filled[job.bank], job.before + 1)

        def freed(eng, job):
            eng.wait_ge(s_freed[job.bank], job.before + 1)

        def bank_free_for(eng, job):
            if not (isinstance(job.before, int) and job.before == 0):
                eng.wait_ge(s_freed[job.bank], job.before)

        def over_chunks(eng, step):
            step(-1)
            step(0)
            step(1)
            with eng.Fori(2, CH - 1) as c:
                step(c)
            step(CH - 1)
            step(CH)

        def slot_of(q, s):
            return SLOT[q * NS + s]

        def pair_bank(q, s, j2):
            return PAIR_BANK[2 * (q * NS + s) + j2]

        def squares_at(k):
            return (th_x[:, :, :], sq_2[:, :, :], xh[:, 0:2, 0:T], xh[:, 2:4, 0:T])[k]

        def early(c, n):
            return isinstance(c, int) and c < n

        @block.sync
        def _(sp):
            small = [
                (in_w, in_wT, "(k p) e -> p k e"), (xproj_w, xproj_wT, "(k p) e -> p k e"),
                (out_w, out_wT, "(k p) e -> p k e"), (conv_ws, conv_w, "(k p) e -> p k e"),
                (a_neg, A_log, "(k p) e -> p k e"),
            ]
            for q in range(NQ):
                sp.dma_start(x_in[:, q, :, :], xT[q, :, 0:T].rearrange("(k p) t -> p k t", p=P)).then_inc(s_x[q], 16)
                for dst, src, how in small:
                    sp.dma_start(dst[:, q, :, :], src[q].rearrange(how, p=P)).then_inc(s_w_small, 16)
                sp.dma_start(dt_w[:, q, :], dt_wT[q]).then_inc(s_w_small, 16)
                for dst, src in ((conv_bs, conv_b), (dt_bs, dt_b), (d_skip, Dp)):
                    sp.dma_start(dst[:, q, :], src[q]).then_inc(s_w_small, 16)
            sp.dma_start(ident[:, :], ident_in).then_inc(s_w_small, 16)
            sp.dma_start(res[:, :, :], x[0:T, :].rearrange("(b p) f -> p b f", p=P)).then_inc(s_res, 16)
            sp.dma_start(gate_w[:, :, :].bitcast(I32), w_gateT.rearrange("(k p) e -> p k e", p=P)).then_inc(s_w_ffn, 16)
            sp.dma_start(up_w[:, :, :].bitcast(I32), w_upT.rearrange("(k p) e -> p k e", p=P)).then_inc(s_w_ffn, 16)
            sp.dma_start(down_w[:, :, :].bitcast(I32), w_downT.rearrange("(k p) e -> p k e", p=P)).then_inc(s_w_ffn, 16)

            def save_b_c(c, q):
                u = 2 * c + q
                freed(sp, MiscJob(c - 1 + q, 1 - q, "P", CH))
                if not early(c, 1):
                    sp.wait_ge(s_dbu, (u - 2) * NS + NS)
                    sp.wait_ge(s_prod, (u - 2) * NS + NS)
                sp.dma_start(bc_scratch[q], dt_sb[R:, :]).then_inc(s_bc_saved, 16)
                sp.wait_ge(s_bc_saved, (u + 1) * 16)

            def load_row(c, q, s, rows, loaded, used, kind):
                if s >= NG or not (early(c, 1) and q == 0):
                    sp.wait_ge(used, (2 * c + q) * NS + s - NG + 1)
                sp.dma_start(rows[:, s % NG, :], bc_scratch[q, kind * NS + s, :].partition_broadcast(P)
                             ).then_inc(loaded[s % NG], 16)

            def load_b(c, q, s):
                load_row(c, q, s, b_rows, s_b_row, s_dbu, 0)

            def load_c(c, q, s):
                load_row(c, q, s, c_rows, s_c_row, s_prod, 1)

            def half(c, q):
                parts = parts_of(2 if not isinstance(c, int) else c, q, CH)
                u = 2 * c + q
                if "scan" in parts:
                    for s in (4, 5):
                        load_b(c, q, s)
                        load_c(c, q, s - 2)
                if q == 0 and not early(c, 2):
                    sp.wait_ge(s_norm, (2 * (c - 2) + 2) * TB)
                    sp.dma_start(out[bass.ds((c - 2) * T, T), :].rearrange("(b p) f -> p b f", p=P),
                                 xn[:, :, :]).then_inc(s_stored, 16)
                if "scan" in parts:
                    for s in (6, 7, 8):
                        load_b(c, q, s)
                        load_c(c, q, s - 2)
                    if not (isinstance(c, int) and c == CH - 1):
                        filled(sp, MiscJob(c, q, "Z1", CH))
                        sp.dma_start(x_in[:, q, :, :],
                                     xT[q, :, bass.ds((c + 1) * T, T)].rearrange("(k p) t -> p k t", p=P)
                                     ).then_inc(s_x[q], 16)
                    for s in (9, 10, 11):
                        load_b(c, q, s)
                        load_c(c, q, s - 2)
                    if q == 0 and not early(c, 1):
                        sp.wait_ge(s_norm, (2 * (c - 1) + 1) * TB)
                        sp.dma_start(res[:, :, :],
                                     x[bass.ds(c * T, T), :].rearrange("(b p) f -> p b f", p=P)).then_inc(s_res, 16)
                    for s in (12, 13, 14, 15):
                        load_b(c, q, s)
                        load_c(c, q, s - 2)
                    load_c(c, q, 14)
                    load_c(c, q, 15)
                if "front" in parts:
                    nxt = (c, 1) if q == 0 else (c + 1, 0)
                    save_b_c(*nxt)
                    for s in range(NG):
                        load_b(*nxt, s)
                        if s >= 2:
                            load_c(*nxt, s - 2)

            def step(c):
                for q in (0, 1):
                    half(c, q)

            over_chunks(sp, step)
            sp.wait_ge(s_norm, 2 * CH * TB)
            sp.dma_start(out[(CH - 1) * T:, :].rearrange("(b p) f -> p b f", p=P), xn[:, :, :]).then_inc(s_stored, 16)
            sp.wait_ge(s_stored, 16 * CH)

        @block.tensor
        def _(pe):
            pe.wait_ge(s_prep, 1)
            pe.wait_ge(s_w_small, 16 * (2 * 9 + 1))

            def mm(out_, lhsT, rhs, k, n):
                return nc.tensor.matmul(out_, lhsT, rhs, start=(k == 0), stop=(k == n - 1), skip_group_check=True)

            def sum_y(c, q, s, back=0):
                u = 2 * c + (q - 2 * back)
                if s + 1 in ADDED[q]:
                    return
                if s in ADDED[q]:
                    pe.wait_ge(s_add, added_before(c, q, s, back) + 1)
                else:
                    pe.wait_ge(s_prod, u * NS + s + 1)
                begins = s == (1 if 1 in ADDED[q] else 0)
                if begins and not (early(c, 1) and q == 0):
                    pe.wait_ge(s_skip, u)
                for j2 in range(2):
                    last = mm(y[:, 2 * j2:2 * j2 + 2, :], ident[:, :],
                              states[:, slot_of(q, s), 2 * j2:2 * j2 + 2, :], 0 if begins else s, NS)
                last.then_inc(s_sum, 1)

            def half(c, hh):
                kc = 2 if not isinstance(c, int) else c
                parts = parts_of(kc, hh, CH)
                u = 2 * c + hh
                qf, qn = 1 - hh, 1 - hh
                un = u + 1

                def job(name):
                    j = MiscJob(c, hh, name, CH)
                    bank_free_for(pe, j)
                    return j

                def project_in(j2, name, q, first, cc):
                    j = job(f"{name}{j2}")
                    pe.wait_ge(s_x[q], 16 * (cc + 1))
                    for i in range(2):
                        e = first + (2 * j2 + i) * P
                        for k in range(KM):
                            last = mm(misc[:, j.bank, i, :], in_w[:, q, k, e:e + P], x_in[:, q, k, :], k, KM)
                    last.then_inc(s_filled[j.bank], 1)

                def project_out():
                    j = job("O")
                    pe.wait_ge(s_gated, u)
                    for b in range(TB):
                        for k in range(DT):
                            last = mm(misc[:, j.bank, b, :], zs[:, k, b * P:(b + 1) * P], out_w[:, qf, k, :], k, DT)
                    last.then_inc(s_filled[j.bank], 1)

                def xproj():
                    j = job("P")
                    pe.wait_ge(s_xc, 2 * un + 2)
                    for k in range(DT):
                        last = mm(misc[0:R + 2 * NS, j.bank, 0, :], xproj_w[:, qn, k, :], xc[:, qn, k, :], k, DT)
                    last.then_inc(s_filled[j.bank], 1)

                def dt_proj(j2):
                    j = job(f"D{j2}")
                    freed(pe, MiscJob(c, hh, "P", CH))
                    for i in range(2):
                        e = (2 * j2 + i) * P
                        last = mm(misc[:, j.bank, i, :], dt_w[:, qn, e:e + P], dt_sb[0:R, :], 0, 1)
                    last.then_inc(s_filled[j.bank], 1)

                def turn_norm(j2):
                    j = job(f"T{j2}")
                    pe.wait_ge(s_norm, (2 * (c - 1) + 1) * TB)
                    for i in range(2):
                        for b in range(TB):
                            k = 2 * j2 + i
                            last = nc.tensor.transpose(misc[:, j.bank, i, b * P:(b + 1) * P],
                                                       xn[:, b, k * P:(k + 1) * P], ident[:, :])
                    last.then_inc(s_filled[j.bank], 1)

                def gate_up(f):
                    j = job(f"G{f}")
                    if f == 0:
                        freed(pe, MiscJob(c, 0, "T1", CH))
                        pe.wait_ge(s_ffn_prep, 3)
                    for i, w in enumerate((gate_w, up_w)):
                        for k in range(KD):
                            last = mm(misc[:, j.bank, i, :], w[:, k, f * P:(f + 1) * P], xnT[:, k, :], k, KD)
                    last.then_inc(s_filled[j.bank], 1)

                def down(b, third):
                    j = MiscJob(c, hh, f"W{b}", CH)
                    if third == 0:
                        bank_free_for(pe, j)
                    for f in range(4 * third, 4 * third + 4):
                        if b == 0:
                            pe.wait_ge(s_hid, FT * (c - 1) + f + 1)
                        last = mm(misc[:, j.bank, :, :], hid[:, f, b * P:(b + 1) * P], down_w[:, f, :], f, FT)
                    if third == 2:
                        last.then_inc(s_filled[j.bank], 1)

                for s in range(NS):
                    if "ffn" in parts and hh == 1 and s < 4:
                        gate_up(s + 6)
                    if "fin" in parts and s == 4:
                        project_out()
                    if "scan" in parts and s in (5, 6):
                        project_in(s - 5, "Z", hh, DI, c)
                    if "front" in parts and s == 7:
                        xproj()
                    if "ffn" in parts and hh == 0 and s == 8:
                        turn_norm(0)
                        turn_norm(1)
                    if "ffn" in parts and hh == 1 and s in (7, 8):
                        gate_up(s + 3)
                    if "front" in parts and s == 9:
                        dt_proj(0)
                        dt_proj(1)
                    if "ffn" in parts and hh == 1 and s >= 10:
                        down((s - 10) // 3, (s - 10) % 3)
                    if "ahead" in parts and s >= 14:
                        project_in(s - 14, "X", hh, 0, c + 1)
                    if "ffn" in parts and hh == 0 and s >= 10:
                        gate_up(s - 10)
                    if s > 0 and "scan" in parts:
                        sum_y(c, hh, s - 1)
                    if s == 0 and "fin" in parts:
                        sum_y(c, qf, NS - 1, back=1 - hh)

            def step(c):
                for hh in (0, 1):
                    half(c, hh)

            over_chunks(pe, step)

        @block.scalar
        def _(act):
            act.wait_ge(s_w_small, 16 * (2 * 9 + 1))
            nc.scalar.activation(a_neg[:, :, :, :], a_neg[:, :, :, :], ACT.Exp).then_inc(s_a, 1)

            def half(c, hh):
                kc = 2 if not isinstance(c, int) else c
                parts = parts_of(kc, hh, CH)
                u = 2 * c + hh
                un = u + 1
                qn = 1 - hh

                def exps(s):
                    i = u * NS + s
                    if s == 0:
                        act.wait_ge(s_delta, 2 * (u + 1))
                    for d in range(DT):
                        at = 2 * (hh * NS + s) + d // 2
                        if d % 2 == 0 and not (early(c, 1) and at < PAIR_BANKS):
                            act.wait_ge(s_scan, 2 * i + d // 2 - uses_back(PAIR_BANK, at) + 1)
                        nc.scalar.activation(dA[:, pair_bank(hh, s, d // 2), d % 2, :], delta[:, hh, d, :], ACT.Exp,
                                             scale=a_neg[:, hh, d, s:s + 1]).then_inc(s_dA, 1)

                def save_carry(uu, q, s):
                    act.wait_ge(s_scan, 2 * (uu * NS + s + 1))
                    nc.scalar.copy(carry[:, q, s, :], states[:, slot_of(q, s), :, T - 1]).then_inc(s_carry, 1)

                def xh_halo():
                    if early(c, 0):
                        act.wait_ge(s_zero, 5 + NF)
                    else:
                        act.wait_ge(s_halo, u + 1)
                    if "front" in parts:
                        act.wait_ge(s_fac, NF * (2 * un + 2))
                    nc.scalar.copy(xh[:, :, 0:TAPS - 1], halo[:, hh, :, :]).then_inc(s_xh, 1)

                def xh_out(j2, uu, job):
                    filled(act, job)
                    act.wait_ge(s_xh, uu + 1)
                    nc.scalar.copy(xh[:, 2 * j2:2 * j2 + 2, TAPS - 1:], misc[:, job.bank, :, :]
                                   ).then_inc(s_freed[job.bank], 1)
                    act.wait_ge(s_freed[job.bank], job.before + 1)

                def save_halo():
                    nc.scalar.copy(halo[:, qn, :, :], xh[:, :, T:T + TAPS - 1]).then_inc(s_halo, 1)

                def taps(i, uu, q):
                    if not (early(c, 0) and hh == 0):
                        act.wait_ge(s_conv, 4 * uu + i)
                    for k in range(TAPS):
                        last = nc.scalar.activation(tmp4[:, k, :], xh[:, i, k:k + T], ACT.Identity,
                                                    bias=conv_bs[:, q, i:i + 1] if k == TAPS - 1 else 0.0,
                                                    scale=conv_ws[:, q, i, k:k + 1])
                    last.then_inc(s_taps, 1)

                def xc_tanh(j2):
                    act.wait_ge(s_conv, 4 * un + 2 * j2 + 2)
                    if not (early(c, 0) and j2 == 0):
                        act.wait_ge(s_xc, 2 * un + j2)
                    nc.scalar.activation(th_x[:, :, :], xh[:, 2 * j2:2 * j2 + 2, 0:T], ACT.Tanh).then_inc(s_xth, 1)

                def dt_b_c_out():
                    j = MiscJob(c, hh, "P", CH)
                    filled(act, j)
                    if not early(c, 0):
                        act.wait_ge(s_bc_saved, 16 * un)
                    nc.scalar.copy(dt_sb[:, :], misc[0:R + 2 * NS, j.bank, 0, :]).then_inc(s_freed[j.bank], 1)

                def delta_terms(j2):
                    j = MiscJob(c, hh, f"D{j2}", CH)
                    filled(act, j)
                    for i in range(2):
                        d = 2 * j2 + i
                        nc.scalar.activation(tmp4[:, d, :], misc[:, j.bank, i, :], ACT.Abs, bias=dt_bs[:, qn, d:d + 1])
                        last = nc.scalar.activation(delta[:, qn, d, :], misc[:, j.bank, i, :], ACT.Relu,
                                                    bias=dt_bs[:, qn, d:d + 1])
                    last.then_inc(s_freed[j.bank], 1)
                    act.wait_ge(s_freed[j.bank], j.before + 1)
                    u_ = tmp4[:, 2 * j2:2 * j2 + 2, :]
                    nc.scalar.activation(u_, u_, ACT.Exp, scale=-1.0).then_inc(s_exp, 1)

                def square(j2, k):
                    u_ = tmp4[:, 2 * j2:2 * j2 + 2, :]
                    if k == 0:
                        act.wait_ge(s_exp, 2 * un + j2 + 1)
                    if j2 == 1:
                        act.wait_ge(s_fac, NF * 2 * un + k + 1)
                    root = LOG1P_LEAD ** 0.5 if k == 0 else 1.0
                    nc.scalar.activation(squares_at(k), u_, ACT.Square, bias=sq_bias[:, k:k + 1], scale=root
                                         ).then_inc(s_sq, 1)

                def z_tanh(j2):
                    j = MiscJob(c, hh, f"Z{j2}", CH)
                    filled(act, j)
                    if j2 == 0 and "fin" in parts:
                        filled(act, MiscJob(c, hh, "O", CH))
                    nc.scalar.activation(zs[:, 2 * j2:2 * j2 + 2, :], misc[:, j.bank, :, :], ACT.Tanh).then_inc(s_zth, 1)

                def norm_apply(which, cc):
                    n = 2 * cc + which
                    act.wait_ge(s_rstd, 4 * (n + 1))
                    if which == 1:
                        dst, src = xn, xn
                    else:
                        dst, src = xn, res
                    if which == 0 and not early(cc, 1):
                        act.wait_ge(s_stored, 16 * cc)
                    for b in range(TB):
                        nc.scalar.activation(dst[:, b, :], src[:, b, :], ACT.Identity, bias=shift[:, which, b:b + 1],
                                             scale=rstd[:, which, b:b + 1]).then_inc(s_norm, 1)

                def turned_norm_out(j2):
                    j = MiscJob(c, hh, f"T{j2}", CH)
                    filled(act, j)
                    nc.scalar.copy(xnT[:, 2 * j2:2 * j2 + 2, :], misc[:, j.bank, :, :]).then_inc(s_freed[j.bank], 1)

                def gate_out(f):
                    cg, hg = (c, 0) if f <= 5 else (c, 1)
                    j = MiscJob(cg, hg, f"G{f}", CH)
                    filled(act, j)
                    if not (early(c, 2) and f < 2):
                        act.wait_ge(s_hid, FT * (c - 1) + f - 1)
                    nc.scalar.copy(up_f[:, f % 2, :], misc[:, j.bank, 1, :])
                    nc.scalar.activation(th_g[:, f % 2, :], misc[:, j.bank, 0, :], ACT.Tanh).then_inc(s_gth, 1)

                for s in range(NS):
                    if "scan" in parts:
                        exps(s)
                        if s > 0:
                            save_carry(u, hh, s - 1)
                    if s == 0 and "fin" in parts:
                        save_carry(u - 1, qn, NS - 1)
                    if "front" in parts:
                        if s == 0:
                            xh_out(1, un, MiscJob(c - 1 + hh, 1 - hh, "X1", CH))
                            save_halo()
                        if s in (1, 2, 3):
                            taps(s, un, qn)
                        if s in (3, 5):
                            xc_tanh((s - 3) // 2)
                        if s == 8:
                            dt_b_c_out()
                    if s == 3 and hh == 0 and not early(c, 2):
                        norm_apply(1, c - 2)
                    if "scan" in parts and s in (6, 7):
                        z_tanh(s - 6)
                    if hh == 0 and "ffn" in parts:
                        if s == 7:
                            norm_apply(0, c - 1)
                        if s == 9:
                            turned_norm_out(0)
                            turned_norm_out(1)
                        if s >= 11:
                            gate_out(s - 11)
                    if hh == 1 and "ffn" in parts:
                        if s < 5:
                            gate_out(s + 5)
                        if s in (8, 9):
                            gate_out(s + 2)
                    if "front" in parts:
                        if s == 10:
                            delta_terms(0)
                            square(0, 0)
                            square(0, 1)
                        if s == 11:
                            square(0, 2)
                            square(0, 3)
                            delta_terms(1)
                        if s in (12, 13):
                            square(1, 2 * s - 24)
                            square(1, 2 * s - 23)
                    if "ahead" in parts and s == 15:
                        xh_halo()
                        xh_out(0, u + 2, MiscJob(c, hh, "X0", CH))
                        taps(0, u + 2, hh)

            def step(c):
                for hh in (0, 1):
                    half(c, hh)

            over_chunks(act, step)
            act.wait_ge(s_rstd, 4 * 2 * CH)
            for b in range(TB):
                nc.scalar.activation(xn[:, b, :], xn[:, b, :], ACT.Identity, bias=shift[:, 1, b:b + 1],
                                     scale=rstd[:, 1, b:b + 1]).then_inc(s_norm, 1)

        @block.gpsimd
        def _(pool):
            nc.gpsimd.memset(carry[:, :, :, :], 0.0).then_inc(s_zero, 1)
            nc.gpsimd.memset(halo[:, :, :, :], 0.0).then_inc(s_zero, 1)
            nc.gpsimd.memset(minus_half[:, :], -0.5).then_inc(s_zero, 1)
            nc.gpsimd.memset(minus_one[:, :], -1.0).then_inc(s_zero, 1)
            nc.gpsimd.memset(eps_c[:, :], EPS).then_inc(s_zero, 1)
            for k, (a, _) in enumerate(LOG1P_FACTORS):
                root = LOG1P_LEAD ** 0.5 if k == 0 else 1.0
                nc.gpsimd.memset(sq_bias[:, k:k + 1], root * a).then_inc(s_zero, 1)
            pool.wait_ge(s_zero, 5 + NF)

            def rstd_steps(n):
                w = n[1]
                k = 2 * n[0] + w
                pool.wait_ge(s_mv, k + 1)
                if not (early(n[0], 1)):
                    pool.wait_ge(s_norm, (k - 2 + 1) * TB)
                nc.gpsimd.tensor_tensor(var_eps[:, w, :], mv[:, w, :, 1], eps_c[:, :], ALU.add).then_inc(s_rstd, 1)
                nc.gpsimd.tensor_tensor(negm[:, w, :], mv[:, w, :, 0], minus_one[:, :], ALU.mult).then_inc(s_rstd, 1)
                pool.wait_ge(s_rstd, 4 * k + 2)
                nc.gpsimd.tensor_tensor(rstd[:, w, :], var_eps[:, w, :], minus_half[:, :], ALU.pow).then_inc(s_rstd, 1)
                pool.wait_ge(s_rstd, 4 * k + 3)
                nc.gpsimd.tensor_tensor(shift[:, w, :], negm[:, w, :], rstd[:, w, :], ALU.mult).then_inc(s_rstd, 1)

            def half(c, hh):
                kc = 2 if not isinstance(c, int) else c
                parts = parts_of(kc, hh, CH)
                u = 2 * c + hh
                un = u + 1
                qn = 1 - hh

                def dbu_of(s):
                    i = u * NS + s
                    if s == 0:
                        pool.wait_ge(s_du, 2 * (u + 1))
                    pool.wait_ge(s_b_row[s % NG], 16 * (NS // NG * u + s // NG + 1))
                    if not (early(c, 1) and hh == 0 and s < SLOTS):
                        at = (hh * NS + s - uses_back(SLOT, hh * NS + s)) % (2 * NS)
                        back, qb, sb_ = int(at > hh * NS + s), at // NS, at % NS
                        if sb_ + 1 in ADDED[qb]:
                            pool.wait_ge(s_add, added_before(c, qb, sb_ + 1, back) + 1)
                        else:
                            pool.wait_ge(s_sum, sums_before(c, qb, sb_, back) + 1)
                    rows = b_rows[:, s % NG, :].unsqueeze(1).broadcast_to([P, DT, T])
                    nc.gpsimd.tensor_tensor(states[:, slot_of(hh, s), :, :], du[:, hh, :, :], rows, ALU.mult
                                            ).then_inc(s_dbu, 1)

                def gate_y():
                    pool.wait_ge(s_skip, u)
                    nc.gpsimd.tensor_tensor(zs[:, :, :], zs[:, :, :], xc[:, qn, :, :], ALU.mult).then_inc(s_gated, 1)

                def conv_add(i):
                    n = 4 * un + i
                    pool.wait_ge(s_taps, n + 1)
                    nc.gpsimd.tensor_tensor(tmp4[:, 0:2, :], tmp4[:, 0:2, :], tmp4[:, 2:4, :], ALU.add).then_inc(s_pairs, 1)
                    pool.wait_ge(s_pairs, n + 1)
                    nc.gpsimd.tensor_tensor(xh[:, i, 0:T], tmp4[:, 0, :], tmp4[:, 1, :], ALU.add).then_inc(s_conv, 1)

                def delta_and_du(j2):
                    pair = slice(2 * j2, 2 * j2 + 2)
                    pool.wait_ge(s_fac, NF * (2 * un + j2 + 1))
                    nc.gpsimd.tensor_tensor(delta[:, qn, pair, :], delta[:, qn, pair, :], du[:, qn, pair, :], ALU.add
                                            ).then_inc(s_delta, 1)
                    pool.wait_ge(s_delta, 2 * un + j2 + 1)
                    nc.gpsimd.tensor_tensor(du[:, qn, pair, :], delta[:, qn, pair, :], xc[:, qn, pair, :], ALU.mult
                                            ).then_inc(s_du, 1)

                def hidden(f, cc, hf):
                    freed(pool, MiscJob(cc, hf, f"G{f}", CH))
                    nc.gpsimd.tensor_tensor(hid[:, f, :], th_g[:, f % 2, :], up_f[:, f % 2, :], ALU.mult).then_inc(s_hid, 1)

                for s in range(NS):
                    if "scan" in parts:
                        dbu_of(s)
                    if "front" in parts and s in (0, 2, 3, 4):
                        conv_add((0, 2, 3, 4).index(s))
                    if s == 3 and hh == 0 and not early(c, 2):
                        rstd_steps((c - 2, 1))
                    if "fin" in parts and s == 3:
                        gate_y()
                    if hh == 1 and "ffn" in parts:
                        if s < 7:
                            hidden(s + 3, c, 0 if s < 3 else 1)
                        if s in (10, 11):
                            hidden(s, c, 1)
                    if hh == 0 and "ffn" in parts:
                        if s == 7:
                            rstd_steps((c - 1, 0))
                        if s >= 13:
                            hidden(s - 13, c, 0)
                    if "front" in parts and s in (14, 15):
                        delta_and_du(s - 14)

            def step(c):
                for hh in (0, 1):
                    half(c, hh)

            over_chunks(pool, step)
            rstd_steps((CH - 1, 1))

        @block.vector
        def _(dve):
            dve.wait_ge(s_w_small, 16 * (2 * 9 + 1))
            nc.vector.tensor_scalar(in_w[:, :, :, DI:], in_w[:, :, :, DI:], 0.5, None, ALU.mult)
            nc.vector.tensor_scalar(conv_ws[:, :, :, :], conv_ws[:, :, :, :], 0.5, None, ALU.mult)
            nc.vector.tensor_scalar(conv_bs[:, :, :], conv_bs[:, :, :], 0.5, None, ALU.mult)
            dve.wait_ge(s_a, 1)
            nc.vector.tensor_scalar(a_neg[:, :, :, :], a_neg[:, :, :, :], -1.0, None, ALU.mult).then_inc(s_prep, 1)
            dve.wait_ge(s_zero, 2)

            def norm_stats(which, cc, src, job):
                k = 2 * cc + which
                freed(dve, job)
                for b in range(TB):
                    nc.vector.bn_stats(stats[:, which, b, :], src[:, b, :]).then_inc(s_stats, 1)
                dve.wait_ge(s_stats, TB * (k + 1))
                if not early(cc, 1):
                    dve.wait_ge(s_rstd, 4 * (k - 2 + 1))
                nc.vector.tensor_copy(pacer[:, :], stats[:, which, 0, 0:1])
                for b in range(TB):
                    last = nc.vector.bn_aggr(mv[:, which, b, :], stats[:, which, b, :])
                last.then_inc(s_mv, 1)

            def down_out(c, hh, b):
                j = MiscJob(c, hh, f"W{b}", CH)
                filled(dve, j)
                nc.vector.tensor_tensor(xn[:, b, :], misc[:, j.bank, :, :].rearrange("p a t -> p (a t)"),
                                        xn[:, b, :], ALU.add).then_inc(s_freed[j.bank], 1)

            def half(c, hh):
                kc = 2 if not isinstance(c, int) else c
                parts = parts_of(kc, hh, CH)
                u = 2 * c + hh
                qn = 1 - hh

                def scan(s, d):
                    i = u * NS + s
                    if d % 2 == 0:
                        dve.wait_ge(s_dA, i * DT + d + 2)
                    if d == 0:
                        dve.wait_ge(s_dbu, i + 1)
                    slot = states[:, slot_of(hh, s), d, :]
                    last = nc.vector.tensor_tensor_scan(slot, dA[:, pair_bank(hh, s, d // 2), d % 2, :], slot, carry[:, hh, s, d:d + 1],
                                                        ALU.mult, ALU.add)
                    if d % 2 == 1:
                        last.then_inc(s_scan, 1)

                def times_c(uu, q, s):
                    i = uu * NS + s
                    dve.wait_ge(s_carry, i + 1)
                    dve.wait_ge(s_c_row[s % NG], 16 * (NS // NG * uu + s // NG + 1))
                    slot = states[:, slot_of(q, s), :, :]
                    rows = c_rows[:, s % NG, :].unsqueeze(1).broadcast_to([P, DT, T])
                    nc.vector.tensor_tensor(slot, slot, rows, ALU.mult).then_inc(s_prod, 1)

                def add_pair(uu, q, s):
                    if s not in ADDED[q]:
                        return
                    dve.wait_ge(s_prod, uu * NS + s + 1)
                    slot = states[:, slot_of(q, s), :, :]
                    nc.vector.tensor_tensor(slot, slot, states[:, slot_of(q, s - 1), :, :], ALU.add).then_inc(s_add, 1)

                def y_skip():
                    dve.wait_ge(s_sum, sums_before(c, qn, NS - 1, back=1 - hh) + 1)
                    for d in range(DT):
                        last = nc.vector.scalar_tensor_tensor(xc[:, qn, d, :], xc[:, qn, d, :], d_skip[:, qn, d:d + 1],
                                                              y[:, d, :], ALU.mult, ALU.add)
                    last.then_inc(s_skip, 1)

                def residual():
                    j = MiscJob(c, hh, "O", CH)
                    filled(dve, j)
                    cf = c - 1 if hh == 0 else c
                    dve.wait_ge(s_res, 16 * (cf + 1))
                    part = res[:, :, qn * DM:(qn + 1) * DM]
                    nc.vector.tensor_tensor(part, misc[:, j.bank, :, :], part, ALU.add).then_inc(s_freed[j.bank], 1)

                def z_silu(j2):
                    j = MiscJob(c, hh, f"Z{j2}", CH)
                    dve.wait_ge(s_zth, 2 * u + j2 + 1)
                    nc.vector.scalar_tensor_tensor(zs[:, 2 * j2:2 * j2 + 2, :], zs[:, 2 * j2:2 * j2 + 2, :], 1.0,
                                                   misc[:, j.bank, :, :], ALU.add, ALU.mult).then_inc(s_freed[j.bank], 1)

                def gate_silu(f):
                    j = MiscJob(c, 0 if f <= 5 else 1, f"G{f}", CH)
                    dve.wait_ge(s_gth, FT * (c - 1) + f + 1)
                    nc.vector.scalar_tensor_tensor(th_g[:, f % 2, :], th_g[:, f % 2, :], 1.0,
                                                   misc[:, j.bank, 0, :], ALU.add, ALU.mult).then_inc(s_freed[j.bank], 1)

                def xc_silu(j2):
                    dve.wait_ge(s_xth, 2 * (u + 1) + j2 + 1)
                    if j2 == 0 and "fin" in parts:
                        dve.wait_ge(s_gated, u)
                    pair = slice(2 * j2, 2 * j2 + 2)
                    nc.vector.scalar_tensor_tensor(xc[:, qn, pair, :], th_x[:, :, :], 1.0, xh[:, pair, 0:T],
                                                   ALU.add, ALU.mult).then_inc(s_xc, 1)

                def factor(j2, k):
                    un = u + 1
                    n = NF * (2 * un + j2) + k
                    dve.wait_ge(s_sq, n + 1)
                    if k > 0:
                        dve.wait_ge(s_fac, n)
                    elif "fin" in parts:
                        dve.wait_ge(s_dbu, u * NS)
                    u_ = tmp4[:, 2 * j2:2 * j2 + 2, :]
                    acc = du[:, qn, 2 * j2:2 * j2 + 2, :]
                    b_ = LOG1P_FACTORS[k][1] * (LOG1P_LEAD if k == 0 else 1.0)
                    nc.vector.scalar_tensor_tensor(acc, squares_at(k), b_, u_ if k == 0 else acc, ALU.add, ALU.mult
                                                   ).then_inc(s_fac, 1)

                for s in range(NS):
                    if "scan" in parts:
                        scan(s, 0)
                        scan(s, 1)
                    if s > 0 and "scan" in parts:
                        times_c(u, hh, s - 1)
                    if s == 0 and "fin" in parts:
                        times_c(u - 1, qn, NS - 1)
                    if "ffn" in parts and hh == 0 and s >= 12:
                        gate_silu(s - 12)
                    if "ffn" in parts and hh == 1:
                        if s < 6:
                            gate_silu(s + 4)
                        if s in (9, 10):
                            gate_silu(s + 1)
                    if s == 1 and hh == 0 and not early(c, 2):
                        down_out(c - 1, 1, 1)
                    if "scan" in parts:
                        scan(s, 2)
                        scan(s, 3)
                        if s > 0:
                            add_pair(u, hh, s - 1)
                    if s == 0 and "fin" in parts:
                        add_pair(u - 1, qn, NS - 1)
                    if s == 1 and "fin" in parts:
                        y_skip()
                    if s == 1 and hh == 0 and not early(c, 2):
                        norm_stats(1, c - 2, xn, MiscJob(c - 1, 1, "W1", CH))
                    if "fin" in parts and s == 5:
                        residual()
                        if hh == 0:
                            norm_stats(0, c - 1, res, MiscJob(c, 0, "O", CH))
                    if "front" in parts and s in (4, 6):
                        xc_silu((s - 4) // 2)
                    if "scan" in parts and s in (7, 8):
                        z_silu(s - 7)
                    if "ffn" in parts and hh == 1 and s == 14:
                        down_out(c, 1, 0)
                    if "front" in parts and s in (11, 12, 13, 14):
                        j2, k = (s - 11) // 2, 2 * ((s - 11) % 2)
                        factor(j2, k)
                        factor(j2, k + 1)
                if isinstance(c, int) and c == 0 and hh == 1:
                    dve.wait_ge(s_w_ffn, 48)
                    for w, scale in ((gate_w, 0.5 * WEIGHT_SCALE), (up_w, WEIGHT_SCALE), (down_w, WEIGHT_SCALE)):
                        nc.vector.tensor_scalar(w[:, :, :], w[:, :, :].bitcast(I32), scale, None, ALU.mult
                                                ).then_inc(s_ffn_prep, 1)

            def step(c):
                for hh in (0, 1):
                    half(c, hh)

            over_chunks(dve, step)
            down_out(CH, 1, 1)
            norm_stats(1, CH - 1, xn, MiscJob(CH, 1, "W1", CH))


def kernel(**inputs):
    import numpy as np
    import concourse.bacc as bacc
    from concourse.bass_utils import run_bass_kernel_spmd

    get = {name.replace("L0_attn_", "").replace("L0_ffn_", ""): np.asarray(a) for name, a in inputs.items()}
    x = get["x"][0]
    dm = x.shape[1] // 2

    def both(name, turn=False):
        return np.stack([get[name + t].T if turn else get[name + t] for t in "12"])

    def per_channel(name):
        return both(name).reshape(2, -1, P).transpose(0, 2, 1)

    arrays = {
        "xT": np.stack([x[:, :dm].T, x[::-1, dm:].T]),
        "x": x,
        "in_wT": both("in_w", True), "conv_w": both("conv_w"), "conv_b": per_channel("conv_b"),
        "xproj_wT": both("xproj_w", True), "dt_wT": both("dt_w", True), "dt_b": per_channel("dt_b"),
        "A_log": both("A_log"), "Dp": per_channel("D"), "out_wT": both("out_w", True),
        "w_gateT": get["w_gate"].T, "w_upT": get["w_up"].T, "w_downT": get["w_down"].T,
        "ident_in": np.eye(P, dtype=np.float32),
    }
    nc = bacc.Bacc("TRN2", target_bir_lowering=False, num_devices=1)
    feeds, args = {}, []
    for name, a in arrays.items():
        a = np.ascontiguousarray(a)
        feeds[f"{name}_dram"] = a
        args.append(nc.dram_tensor(f"{name}_dram", a.shape, mybir.dt.from_np(a.dtype), kind="ExternalInput").ap())
    out = nc.dram_tensor("out_dram", x.shape, F32, kind="ExternalOutput").ap()
    mamba_pair_ffn_kernel(nc, *args, out)
    r = run_bass_kernel_spmd(nc, [feeds], core_ids=[0])
    return r.results[0]["out_dram"].reshape(1, *x.shape)
```
